# Optimizing a Trainium2 kernel written in Bass

```python
import numpy as np
import jax
import jax.numpy as jnp

def _softmax(x, axis=-1):
    return jax.nn.softmax(x, axis=axis)

def _gelu(x):
    return jax.nn.gelu(x, approximate=True)

def _silu(x):
    return jax.nn.silu(x)

def _sigmoid(x):
    return jax.nn.sigmoid(x)

def _layernorm(x, axis=-1, eps=1e-05):
    m = jnp.mean(x, axis=axis, keepdims=True)
    v = jnp.var(x, axis=axis, keepdims=True)
    return (x - m) / jnp.sqrt(v + eps)

def _scatter_add(tgt, idx, src, axis=0):
    return tgt.at[idx].add(src)

def _segment_sum(src, seg, n):
    return jax.ops.segment_sum(src, seg, n)
kernel_name = 'mk_seq_postln_d1_jaxref_r8_512cad'

def setup_inputs(seed: int=0):
    np.random.seed(seed)
    _w = jnp.asarray

    def _L0_attn_setup():
        import jax, jax.numpy as jnp
        import numpy as np
        import math
        N_HEADS = 8

        def _head_dirs():
            t = np.array([[(i >> 2 & 1) * 2 - 1, (i >> 1 & 1) * 2 - 1, (i & 1) * 2 - 1] for i in range(8)], dtype=np.float32)
            return jnp.asarray(t / np.sqrt(3.0, dtype=np.float32))
        key = jax.random.key(seed)
        k1, k2, k3, k4 = jax.random.split(key, 4)
        B, T, C = (2, 256, 128)
        x = jax.random.normal(k1, (B, T, C), dtype=jnp.float32)
        w_qkv = jax.random.normal(k2, (C, 3 * C), dtype=jnp.float32) * (1.0 / math.sqrt(C))
        w_out = jax.random.normal(k3, (C, C), dtype=jnp.float32) * (1.0 / math.sqrt(C))
        head_scales = jax.random.normal(k4, (N_HEADS,), dtype=jnp.float32) * 0.1
        return {'x': x, 'w_qkv': w_qkv, 'w_out': w_out, 'head_scales': head_scales}
    _L0_attn_in = _L0_attn_setup()

    def _L0_ffn_setup():
        import jax, jax.numpy as jnp
        import numpy as np
        D_MODEL = 128
        N_HEADS = 16
        HEAD_DIM = D_MODEL // N_HEADS
        KV_LATENT = 64
        N_EXPERTS = 4
        D_HIDDEN = 4 * D_MODEL
        B, T = (2, 128)

        def rmsnorm(x, w, eps=1e-06):
            return w * (x * jax.lax.rsqrt(jnp.mean(x * x, axis=-1, keepdims=True) + eps))

        def layernorm(x, g, b, eps=1e-05):
            mu = jnp.mean(x, axis=-1, keepdims=True)
            var = jnp.mean((x - mu) ** 2, axis=-1, keepdims=True)
            return (x - mu) * jax.lax.rsqrt(var + eps) * g + b

        def apply_rope(x):
            t, d = (x.shape[2], x.shape[3])
            half = d // 2
            pos = jnp.arange(t, dtype=x.dtype)[:, None]
            inv_freq = 1.0 / 10000.0 ** (jnp.arange(half, dtype=x.dtype) / half)
            ang = pos * inv_freq[None, :]
            sin, cos = (jnp.sin(ang), jnp.cos(ang))
            x1, x2 = (x[..., :half], x[..., half:])
            return jnp.concatenate([x1 * cos - x2 * sin, x1 * sin + x2 * cos], axis=-1)

        def mla_attention(x, Wq, Wdkv, Wuk, Wuv, Wo, ln_g, ln_b):
            b, t, _ = x.shape
            q = (x @ Wq.T).reshape(b, t, N_HEADS, HEAD_DIM).transpose(0, 2, 1, 3)
            latent = layernorm(x @ Wdkv.T, ln_g, ln_b)
            k = (latent @ Wuk.T).reshape(b, t, N_HEADS, HEAD_DIM).transpose(0, 2, 1, 3)
            v = (latent @ Wuv.T).reshape(b, t, N_HEADS, HEAD_DIM).transpose(0, 2, 1, 3)
            q = apply_rope(q)
            k = apply_rope(k)
            scores = jnp.einsum('bhqd,bhkd->bhqk', q, k) / np.sqrt(HEAD_DIM)
            causal = jnp.tril(jnp.ones((t, t), dtype=bool))
            scores = jnp.where(causal, scores, -jnp.inf)
            attn = jax.nn.softmax(scores, axis=-1)
            out = jnp.einsum('bhqk,bhkd->bhqd', attn, v).transpose(0, 2, 1, 3).reshape(b, t, D_MODEL)
            return out @ Wo.T

        def moe(x, gate_w, gate_b, W1, b1, W2, b2):
            logits = x @ gate_w.T + gate_b
            top = jnp.argmax(logits, axis=-1)
            onehot = jax.nn.one_hot(top, N_EXPERTS, dtype=x.dtype)
            h = jax.nn.relu(jnp.einsum('btd,ehd->bteh', x, W1) + b1)
            y = jnp.einsum('bteh,edh->bted', h, W2) + b2
            return jnp.einsum('bted,bte->btd', y, onehot)
        key = jax.random.key(seed)
        ks = jax.random.split(key, 16)
        s = lambda fan_in: 1.0 / np.sqrt(fan_in)
        return {'x': jax.random.normal(ks[0], (B, T, D_MODEL), jnp.float32), 'norm1_w': jnp.ones((D_MODEL,), jnp.float32), 'norm2_w': jnp.ones((D_MODEL,), jnp.float32), 'Wq': jax.random.normal(ks[1], (D_MODEL, D_MODEL), jnp.float32) * s(D_MODEL), 'Wdkv': jax.random.normal(ks[2], (KV_LATENT, D_MODEL), jnp.float32) * s(D_MODEL), 'Wuk': jax.random.normal(ks[3], (D_MODEL, KV_LATENT), jnp.float32) * s(KV_LATENT), 'Wuv': jax.random.normal(ks[4], (D_MODEL, KV_LATENT), jnp.float32) * s(KV_LATENT), 'Wo': jax.random.normal(ks[5], (D_MODEL, D_MODEL), jnp.float32) * s(D_MODEL), 'ln_g': jnp.ones((KV_LATENT,), jnp.float32), 'ln_b': jnp.zeros((KV_LATENT,), jnp.float32), 'gate_w': jax.random.normal(ks[6], (N_EXPERTS, D_MODEL), jnp.float32) * s(D_MODEL), 'gate_b': jnp.zeros((N_EXPERTS,), jnp.float32), 'W1': jax.random.normal(ks[7], (N_EXPERTS, D_HIDDEN, D_MODEL), jnp.float32) * s(D_MODEL), 'b1': jnp.zeros((N_EXPERTS, D_HIDDEN), jnp.float32), 'W2': jax.random.normal(ks[8], (N_EXPERTS, D_MODEL, D_HIDDEN), jnp.float32) * s(D_HIDDEN), 'b2': jnp.zeros((N_EXPERTS, D_MODEL), jnp.float32)}
    _L0_ffn_in = _L0_ffn_setup()
    _d = {'L0_attn_x': _L0_attn_in['x'], 'L0_attn_w_qkv': _L0_attn_in['w_qkv'], 'L0_attn_w_out': _L0_attn_in['w_out'], 'L0_attn_head_scales': _L0_attn_in['head_scales'], 'L0_ffn_norm1_w': _L0_ffn_in['norm1_w'], 'L0_ffn_norm2_w': _L0_ffn_in['norm2_w'], 'L0_ffn_Wq': _L0_ffn_in['Wq'], 'L0_ffn_Wdkv': _L0_ffn_in['Wdkv'], 'L0_ffn_Wuk': _L0_ffn_in['Wuk'], 'L0_ffn_Wuv': _L0_ffn_in['Wuv'], 'L0_ffn_Wo': _L0_ffn_in['Wo'], 'L0_ffn_ln_g': _L0_ffn_in['ln_g'], 'L0_ffn_ln_b': _L0_ffn_in['ln_b'], 'L0_ffn_gate_w': _L0_ffn_in['gate_w'], 'L0_ffn_gate_b': _L0_ffn_in['gate_b'], 'L0_ffn_W1': _L0_ffn_in['W1'], 'L0_ffn_b1': _L0_ffn_in['b1'], 'L0_ffn_W2': _L0_ffn_in['W2'], 'L0_ffn_b2': _L0_ffn_in['b2']}
    _x0 = _d['L0_attn_x']
    _d['L0_attn_x'] = jax.random.normal(jax.random.fold_in(jax.random.key(seed), 1), (2, 1024, 128), dtype=_x0.dtype)
    del _x0
    return _d

def reference(L0_attn_x, L0_attn_w_qkv, L0_attn_w_out, L0_attn_head_scales, L0_ffn_norm1_w, L0_ffn_norm2_w, L0_ffn_Wq, L0_ffn_Wdkv, L0_ffn_Wuk, L0_ffn_Wuv, L0_ffn_Wo, L0_ffn_ln_g, L0_ffn_ln_b, L0_ffn_gate_w, L0_ffn_gate_b, L0_ffn_W1, L0_ffn_b1, L0_ffn_W2, L0_ffn_b2):

    def _L0_attn_ref(x, w_qkv, w_out, head_scales):
        import jax, jax.numpy as jnp
        import numpy as np
        import math
        N_HEADS = 8

        def _head_dirs():
            t = np.array([[(i >> 2 & 1) * 2 - 1, (i >> 1 & 1) * 2 - 1, (i & 1) * 2 - 1] for i in range(8)], dtype=np.float32)
            return jnp.asarray(t / np.sqrt(3.0, dtype=np.float32))
        B, T, C = x.shape
        H = N_HEADS
        hd = C // H
        scale = 1.0 / math.sqrt(hd)
        dirs = _head_dirs()
        qkv = (x @ w_qkv).reshape(B, T, 3, H, hd)
        q = jnp.transpose(qkv[:, :, 0], (0, 2, 1, 3))
        k = jnp.transpose(qkv[:, :, 1], (0, 2, 1, 3))
        v = jnp.transpose(qkv[:, :, 2], (0, 2, 1, 3))
        scores = jnp.einsum('bhqd,bhkd->bhqk', q, k) * scale
        causal = jnp.tril(jnp.ones((T, T), dtype=bool))
        scores = jnp.where(causal[None, None], scores, -jnp.inf)
        q_proj = jnp.einsum('bhtd,hd->bht', q[..., :3], dirs)
        k_proj = jnp.einsum('bhtd,hd->bht', k[..., :3], dirs)
        geo = q_proj[..., :, None] * k_proj[..., None, :]
        scores = scores + head_scales[None, :, None, None] * geo
        attn = jax.nn.softmax(scores, axis=-1)
        out = jnp.einsum('bhqk,bhkd->bqhd', attn, v).reshape(B, T, C)
        return out @ w_out

    def _L0_ffn_ref(x, norm1_w, norm2_w, Wq, Wdkv, Wuk, Wuv, Wo, ln_g, ln_b, gate_w, gate_b, W1, b1, W2, b2):
        import jax, jax.numpy as jnp
        import numpy as np
        D_MODEL = 128
        N_HEADS = 16
        HEAD_DIM = D_MODEL // N_HEADS
        KV_LATENT = 64
        N_EXPERTS = 4
        D_HIDDEN = 4 * D_MODEL
        B, T = (2, 128)

        def rmsnorm(x, w, eps=1e-06):
            return w * (x * jax.lax.rsqrt(jnp.mean(x * x, axis=-1, keepdims=True) + eps))

        def layernorm(x, g, b, eps=1e-05):
            mu = jnp.mean(x, axis=-1, keepdims=True)
            var = jnp.mean((x - mu) ** 2, axis=-1, keepdims=True)
            return (x - mu) * jax.lax.rsqrt(var + eps) * g + b

        def apply_rope(x):
            t, d = (x.shape[2], x.shape[3])
            half = d // 2
            pos = jnp.arange(t, dtype=x.dtype)[:, None]
            inv_freq = 1.0 / 10000.0 ** (jnp.arange(half, dtype=x.dtype) / half)
            ang = pos * inv_freq[None, :]
            sin, cos = (jnp.sin(ang), jnp.cos(ang))
            x1, x2 = (x[..., :half], x[..., half:])
            return jnp.concatenate([x1 * cos - x2 * sin, x1 * sin + x2 * cos], axis=-1)

        def mla_attention(x, Wq, Wdkv, Wuk, Wuv, Wo, ln_g, ln_b):
            b, t, _ = x.shape
            q = (x @ Wq.T).reshape(b, t, N_HEADS, HEAD_DIM).transpose(0, 2, 1, 3)
            latent = layernorm(x @ Wdkv.T, ln_g, ln_b)
            k = (latent @ Wuk.T).reshape(b, t, N_HEADS, HEAD_DIM).transpose(0, 2, 1, 3)
            v = (latent @ Wuv.T).reshape(b, t, N_HEADS, HEAD_DIM).transpose(0, 2, 1, 3)
            q = apply_rope(q)
            k = apply_rope(k)
            scores = jnp.einsum('bhqd,bhkd->bhqk', q, k) / np.sqrt(HEAD_DIM)
            causal = jnp.tril(jnp.ones((t, t), dtype=bool))
            scores = jnp.where(causal, scores, -jnp.inf)
            attn = jax.nn.softmax(scores, axis=-1)
            out = jnp.einsum('bhqk,bhkd->bhqd', attn, v).transpose(0, 2, 1, 3).reshape(b, t, D_MODEL)
            return out @ Wo.T

        def moe(x, gate_w, gate_b, W1, b1, W2, b2):
            logits = x @ gate_w.T + gate_b
            top = jnp.argmax(logits, axis=-1)
            onehot = jax.nn.one_hot(top, N_EXPERTS, dtype=x.dtype)
            h = jax.nn.relu(jnp.einsum('btd,ehd->bteh', x, W1) + b1)
            y = jnp.einsum('bteh,edh->bted', h, W2) + b2
            return jnp.einsum('bted,bte->btd', y, onehot)
        x = x + mla_attention(rmsnorm(x, norm1_w), Wq, Wdkv, Wuk, Wuv, Wo, ln_g, ln_b)
        x = x + moe(rmsnorm(x, norm2_w), gate_w, gate_b, W1, b1, W2, b2)
        return x
    x = L0_attn_x
    x = _layernorm(x + _L0_attn_ref(x, L0_attn_w_qkv, L0_attn_w_out, L0_attn_head_scales), axis=-1)
    x = _layernorm(x + _L0_ffn_ref(x, L0_ffn_norm1_w, L0_ffn_norm2_w, L0_ffn_Wq, L0_ffn_Wdkv, L0_ffn_Wuk, L0_ffn_Wuv, L0_ffn_Wo, L0_ffn_ln_g, L0_ffn_ln_b, L0_ffn_gate_w, L0_ffn_gate_b, L0_ffn_W1, L0_ffn_b1, L0_ffn_W2, L0_ffn_b2), axis=-1)
    return x

_drawn_inputs = setup_inputs


def setup_inputs(seed=0):
    import zlib

    import numpy as np

    out = dict(_drawn_inputs(seed))
    spreads = {'L0_ffn_norm1_w': (1.0, 0.2),
     'L0_ffn_norm2_w': (1.0, 0.2),
     'L0_ffn_ln_g': (1.0, 0.2),
     'L0_ffn_ln_b': (0.0, 0.1),
     'L0_ffn_gate_b': (0.0, 0.1),
     'L0_ffn_b1': (0.0, 0.1),
     'L0_ffn_b2': (0.0, 0.1)}
    factors = {}
    for name, (base, spread) in spreads.items():
        noise = np.random.default_rng([zlib.crc32(name.encode()), seed]).standard_normal(out[name].shape)
        drawn = base * np.exp(spread * noise) if base else spread * noise
        out[name] = jnp.asarray(drawn.astype(out[name].dtype))
    for name, factor in factors.items():
        out[name] = (out[name] * factor).astype(out[name].dtype)
    return out
```

```python
from contextlib import ExitStack

import numpy as np

import concourse.bass as bass
from concourse import mybir

F32 = mybir.dt.float32
BF16 = mybir.dt.bfloat16
ALU = mybir.AluOpType
ACT = mybir.ActivationFunctionType
AX_X = mybir.AxisListType.X

P = 128
B, T, C = 2, 1024, 128
NT = B * T // P
TB = T // P
NB = B * T // 512
HG = 4
VW = 32
E, HID = 4, 512
HC = HID // P
LAT = 64
SLOTS = 3
PSLOTS = 4
NEG = -1.0e30


class Attention:

    def __init__(self, n, hd, products, scale):
        self.n, self.hd, self.products, self.scale = n, hd, products, scale
        self.heads = C // hd
        self.gb = self.heads // HG
        self.groups = B * self.gb
        self.gw = HG * hd
        self.kprod = len(products) * hd
        self.kmax = 96
        self.kexp = self.kmax + 3


ATT = [Attention(0, 16, [(0, 0), (0, 1), (1, 0), (1, 1), (0, 2), (2, 0)], 16 ** -0.5),
       Attention(1, 8, [(0, 0), (0, 1), (1, 0), (1, 1), (0, 2), (2, 0), (1, 2), (2, 1)], 8 ** -0.5)]


def exp_steps():
    out = []
    for qb in range(T // 512):
        for j in [*range(4 * qb, 4 * qb + 4), *range(4 * qb)]:
            lo = max(0, (j - 4 * qb) * P)
            out.append((qb, j, lo, 512 - lo, j >= 4 * qb))
    return out


STEPS = exp_steps()
NS = len(STEPS)


def exp_units():
    out = []
    for s, (_, _, _, n, _) in enumerate(STEPS):
        out += [(s, 0, 4)] if n <= 256 else [(s, 0, 2), (s, 2, 2)]
    return out


UNITS = exp_units()
NU = len(UNITS)
FIRST_UNIT = [min(v for v in range(NU) if UNITS[v][0] == s) for s in range(NS)]
LAST_UNIT = [max(v for v in range(NU) if UNITS[v][0] == s) for s in range(NS)]
MASKED = [v for v in range(NU) if STEPS[UNITS[v][0]][4]]
NM = len(MASKED)


def max_units():
    out = []
    for i in range(TB):
        for c in range(i // 4 + 1):
            w = min(512, (i + 1) * P - 512 * c)
            nh = min(HG, 512 // w)
            out += [(i, c, h, nh, w) for h in range(0, HG, nh)]
    return out


MAXES = max_units()
NX = len(MAXES)
assert NX % 2 == 0 and NU % 2 == 0 and NS % PSLOTS == 0
LAG = 2
SPREAD = 0.86


END = [max(s for s in range(NS) if STEPS[s][0] == qb) for qb in range(T // 512)]


def events(first, last):
    base = []
    for s in range(NS):
        n = STEPS[s][3]
        base += [(("scores", v, 0), UNITS[v][2] * n) for v in range(NU) if UNITS[v][0] == s]
        if s >= LAG:
            base.append((("pv", s - LAG, 0), 4 * STEPS[s - LAG][3]))
        elif not first:
            base.append((("pv", s - LAG + NS, -1), 4 * 512))
        if s == LAG + 1 and not first:
            base.append((("turn", 1, -1), 0))
        if s == END[0] + LAG + 2:
            base.append((("turn", 0, 0), 0))
    if last:
        base += [(("pv", s, 0), 0) for s in range(NS - LAG, NS)] + [(("turn", 1, 0), 0)]
        return [e for e, _ in base]
    until = sum(w for _, w in base) * SPREAD
    out, done, passed = [], 0, 0
    for e, w in base:
        out.append(e)
        passed += w
        upto = min(NX, int(NX * passed / until))
        out += [("max", u, 0) for u in range(done, upto)]
        if done < NX <= upto:
            waiting = 2
        elif upto == NX and waiting:
            waiting -= 1
            if not waiting:
                out.append(("turnmax", 0, 0))
        done = upto
    return out


def turn_index(kind, q, g, dg):
    base = 3 * g
    if kind == "turn" and dg == -1:
        return base
    if kind == "turn" and q == 0:
        return base + 1
    if kind == "turnmax":
        return base + 2
    return base + 2


def build(nc, a, out):
    ctx = ExitStack()
    with ctx:
        def sb(name, shape, dt=F32):
            return ctx.enter_context(nc.sbuf_tensor(name, shape, dt))

        def sem(name):
            return ctx.enter_context(nc.semaphore(name))

        ps = ctx.enter_context(nc.psum_tensor("ps", [P, 8, 512], F32))
        MAXB, TURNB, PVB = 6, 5, 4

        ident = sb("ident", [P, P])
        identb = sb("identb", [P, P], BF16)
        cmask = sb("cmask", [P, HG, P], BF16)
        eps5 = sb("eps5", [P, 1])
        eps6 = sb("eps6", [P, 1])
        w_qkv = sb("w_qkv", [P, 3 * C])
        w_out = sb("w_out", [P, C])
        hs = sb("hs", [P, 8])
        sign = sb("sign", [P, 8, 3])
        geo = sb("geo", [P, 8, 3])
        geot = sb("geot", [P, 8])
        geou = sb("geou", [P, 8])
        wk = sb("wk", [P, C])
        norm_w = sb("norm_w", [P, 2])
        wq2 = sb("wq2", [P, 2, C])
        wdkv = sb("wdkv", [P, LAT])
        wuk = sb("wuk", [LAT, 2, C])
        wuv = sb("wuv", [LAT, C])
        wo = sb("wo", [P, C])
        ln_gb = sb("ln_gb", [LAT, 2])
        gate_w = sb("gate_w", [P, E])
        gate_b = sb("gate_b", [P, E])
        cos = sb("cos", [P, T])
        sin = sb("sin", [P, T])
        w1 = sb("w1", [P, E * HID])
        b1 = sb("b1", [P, E * HC])
        w2 = sb("w2", [P, E * HC, C])
        b2s = sb("b2s", [1, 3, E * C], BF16)
        b2p = sb("b2p", [3, E * C], BF16)
        ones3 = sb("ones3", [3, P], BF16)

        x0 = sb("x0", [P, NT, C])
        x1 = sb("x1", [P, NT, C])
        xn = sb("xn", [P, NT, C])
        feat = sb("feat", [P, B * T])
        latT = sb("latT", [LAT, B * T])
        att = sb("att", [P, TB, B * C])
        stats = sb("stats", [P, NT, 6])
        mv = sb("mv", [P, NT, 2])
        rstd = sb("rstd", [P, 4, NT])
        parts = sb("parts", [P, 4, 3, 512], BF16)
        vall = sb("vall", [P, B * T])

        qs = sb("qs", [P, SLOTS, HG, T], BF16)
        ks = sb("ks", [P, SLOTS, HG, T], BF16)
        vs = sb("vs", [P, SLOTS, TB, HG * VW])
        pr = sb("pr", [P, PSLOTS, HG, 512])
        rest = pr[:, 3, 2:4, :]
        rope = pr[:, 0:2, 0:3, :]
        lat = pr[:, 2, 0:2, :].rearrange("p a (t l) -> p (a t) l", l=LAT)
        b2 = latT[0:1, 0:E * C]
        b2r = lat[0:1, 0:E * C // LAT, :].rearrange("a t l -> a (t l)")
        ot = sb("ot", [P, 2, 512])
        rc = sb("rc", [P, 2, 4, HG])
        mparts = sb("mparts", [P, SLOTS, HG, TB, 2])
        nmax = sb("nmax", [P, SLOTS, HG * TB])
        nrow = sb("nrow", [HG * TB, 2, P])
        nparts = sb("nparts", [HG * TB, SLOTS, 3, P], BF16)

        hid = pr
        logit = sb("logit", [P, NT, E])
        lmax = sb("lmax", [P, NT])
        eq = sb("eq", [P, NT, E])
        onehot = sb("onehot", [P, NT, E])
        used = sb("used", [P, 2, NT])

        scr = [[nc.dram_tensor(f"scr{n}{k}", [3, B, C, T], BF16, kind="Internal").ap() for k in "qk"]
               for n in range(2)]

        x_in = [sem(f"x_in{n}") for n in range(NB)]
        wqkv_in, geo_in, w_in, cs_in, moe_in = (sem(n) for n in ("wqkv_in", "geo_in", "w_in", "cs_in", "moe_in"))
        made = sem("made")
        dchain, gchain = sem("dchain"), sem("gchain")
        wk_made, wr_made, b2_split, b2_in = (sem(n) for n in ("wk_made", "wr_made", "b2_split", "b2_in"))
        ft_ps, ft_done = sem("ft_ps"), sem("ft_done")
        S = []
        for n in range(2):
            S.append({k: sem(f"{k}{n}") for k in (
                "proj", "hi", "r1", "mid", "lo", "rope_t", "rope_q", "v_ps", "v_done", "v_copied", "ones_made", "p_seen",
                "st_ready", "p_ready", "pm_ready", "pv_done", "ev_ready", "mx_ready", "mx_free",
                "nm_ready", "tp_ready", "tp_free", "ns_hi", "ns_mid", "np_ready", "rows_in", "rc_done",
                "at_done", "y_ps", "y_done", "ssq_in", "ssq_out", "ss_ready", "rms_sq", "hat_done")}
                | {k: [sem(f"{k}{n}_{i}") for i in range(m)] for k, m in (
                    ("stored", 4), ("qk_in", SLOTS))})
        lat_ps, lat_done, latt_ps, latt_done = (sem(n) for n in ("lat_ps", "lat_done", "latt_ps", "latt_done"))
        var_ready = [sem(f"var_ready{n}") for n in range(3)]
        root_done = [sem(f"root_done{n}") for n in range(3)]
        x1_done, lat_stats, x12_done = sem("x1_done"), sem("lat_stats"), sem("x12_done")
        gl_ps, gl_read = sem("gl_ps"), sem("gl_read")
        h_ps, h_act, h_dve, y2_ps, y2_acc, y2_free = (sem(n) for n in ("h_ps", "h_act", "h_dve", "y2_ps", "y2_acc", "y2_free"))
        fin_done, out_done = sem("fin_done"), sem("out_done")

        block = ctx.enter_context(nc.Block())

        def need(eng, sem, value):
            if not (isinstance(value, int) and value <= 0):
                eng.wait_ge(sem, value)

        def over_groups(eng, at, step):
            step(0, 0, 0, True, False)
            rounds = (at.groups - 2) // SLOTS
            if rounds > 1:
                assert rounds * SLOTS == at.groups - 2
                with eng.Fori(0, rounds) as p:
                    for r in range(1, SLOTS + 1):
                        step(p * SLOTS + r, r, p + r // SLOTS, False, False)
            else:
                for g in range(1, at.groups - 1):
                    step(g, g, g // SLOTS, False, False)
            step(at.groups - 1, at.groups - 1, (at.groups - 1) // SLOTS, False, True)

        def scores_at(v):
            s, _, nh = UNITS[v]
            n, b = STEPS[s][3], 2 * (v % 2)
            if nh == 2:
                return ps[:, b:b + 2, 0:n]
            return ps[:, b:b + 2, :].rearrange("p b n -> p (b n)")[:, 0:nh * n].rearrange("p (h n) -> p h n", h=nh)

        def by_group(t, at):
            return t[:, :].rearrange("p (g i w) -> p g i w", g=at.groups, i=TB)

        def turned(at):
            return ps[:, TURNB, :].rearrange("p (t h v) -> p t h v", t=4, h=HG)

        @block.sync
        def _(sp):
            x_view = a["x"].rearrange("b (t p) c -> p (b t) c", p=P)
            for n in range(NB):
                sp.dma_start(x0[:, 4 * n:4 * n + 4, :], x_view[:, 4 * n:4 * n + 4, :]).then_inc(x_in[n], 16)
                if n == 0:
                    sp.dma_start(w_qkv[:, :], a["w_qkv"]).then_inc(wqkv_in, 16)
                    sp.dma_start(hs[:, :], a["hs"]).then_inc(geo_in, 16)
                    sp.dma_start(sign[:, :, :], a["sign"].rearrange("p (h j) -> p h j", j=3)).then_inc(geo_in, 16)
            for dst, src in [(w_out[:, :], "w_out"), (wq2[:, 0, :], "WqT"), (wdkv[:, :], "WdkvT"),
                             (wuk[:, 0, :], "WukT"), (wuv[:, :], "WuvT"), (wo[:, :], "WoT"),
                             (norm_w[:, 0:1], "norm1"), (norm_w[:, 1:2], "norm2"),
                             (ln_gb[:, 0:1], "ln_g"), (ln_gb[:, 1:2], "ln_b"),
                             (gate_w[:, :], "gateT"), (gate_b[:, :], "gate_b")]:
                sp.dma_start(dst, a[src]).then_inc(w_in, 16)
            sp.dma_start(b2[:, :], a["b2"]).then_inc(b2_in, 16)

            def store(at, m):
                s, n = S[at.n], m % NB
                sp.wait_ge(s["lo"], m + 1)
                dst = scr[at.n][m // NB][:, n // 2, :, (n % 2) * 512:(n % 2) * 512 + 512]
                sp.dma_start(dst.rearrange("a c t -> c a t"), parts[:, m % 4, :, :]).then_inc(s["stored"][m % 4], 16)

            def load(at, g):
                hd, gw = at.hd, at.gw
                for k, dst in enumerate((qs, ks)):
                    for j, pair in enumerate(at.products):
                        src = scr[at.n][k][pair[k]].rearrange("b c t -> (b c) t")[g * gw:(g + 1) * gw, :]
                        sp.dma_start(dst[j * hd:(j + 1) * hd, g % SLOTS, :, :],
                                     src.rearrange("(h d) t -> d h t", d=hd)).then_inc(S[at.n]["qk_in"][g % SLOTS], 16)

            def rows(at, g):
                sp.wait_ge(S[at.n]["np_ready"], g + 1)
                for p in range(3):
                    sp.dma_start(qs[at.kmax + p:at.kmax + p + 1, g % SLOTS, :, :].rearrange("a h t -> a (h t)"),
                                 nparts[:, g % SLOTS, p, :]).then_inc(S[at.n]["rows_in"], 16)

            for at in ATT:
                s = S[at.n]
                for m in range(2 * NB):
                    store(at, m)
                for i in range(4):
                    sp.wait_ge(s["stored"][i], 32)
                for g in range(SLOTS):
                    load(at, g)
                rows(at, 0)
                if at.n == 0:
                    sp.dma_start(cos[:, :], a["cos"]).then_inc(cs_in, 16)
                    sp.dma_start(sin[:, :], a["sin"]).then_inc(cs_in, 16)
                    for dst, src in [(w1[:, :], "W1T"), (w2[:, :, :], "W2T"), (b1[:, :], "b1T")]:
                        sp.dma_start(dst, a[src]).then_inc(moe_in, 16)
                    sp.wait_ge(b2_split, 3)
                    for p in range(3):
                        sp.dma_start(b2p[p:p + 1, :], b2s[:, p, :]).then_inc(moe_in, 16)
                for g in range(at.groups - 1):
                    if g >= 1 and g + 2 < at.groups:
                        sp.wait_ge(s["st_ready"], g * NU)
                        load(at, g + 2)
                    rows(at, g + 1)

            o_view = out.rearrange("b (t p) c -> p (b t) c", p=P)
            for n in range(NB):
                sp.wait_ge(fin_done, n + 1)
                sp.dma_start(o_view[:, 4 * n:4 * n + 4, :], xn[:, 4 * n:4 * n + 4, :]).then_inc(out_done, 16)
            sp.wait_ge(out_done, 16 * NB)

        @block.gpsimd
        def _(pool):
            pool.memset(ident[:, :], 0.0).then_inc(gchain, 1)
            pool.memset(identb[:, :], 0.0).then_inc(gchain, 1)
            pool.memset(cmask[:, :, :], 0.0).then_inc(gchain, 1)
            pool.wait_ge(gchain, 3)
            for t in (ident, identb):
                pool.affine_select(out=t[:, :], in_=t[:, :], compare_op=ALU.not_equal, fill=1.0,
                                   base=0, pattern=[[-1, P]], channel_multiplier=1).then_inc(made, 1)
            pool.affine_select(out=cmask[:, :, :], in_=cmask[:, :, :], compare_op=ALU.is_ge, fill=NEG,
                               base=0, pattern=[[0, HG], [-1, P]], channel_multiplier=1).then_inc(made, 1)
            pool.memset(eps5[:, :], 1e-5).then_inc(made, 1)
            pool.memset(eps6[:, :], 1e-6).then_inc(made, 1)
            pool.memset(mparts[:, :, :, 0:4, 1], -3.0e38).then_inc(made, 1)
            pool.wait_ge(made, 6)
            pool.memset(ones3[:, :], 1.0).then_inc(made, 1)
            pool.wait_ge(made, 7)

            def pads(at, n):
                for slot in range(SLOTS):
                    v = vs[:, slot, :, :].rearrange("p t (h v) -> p t h v", v=VW)
                    pool.memset(v[:, :, :, at.hd + 1:VW], 0.0).then_inc(S[n]["ones_made"], 1)
                    pool.memset(v[:, :, :, at.hd:at.hd + 1], 1.0).then_inc(S[n]["ones_made"], 1)
                    pool.wait_ge(S[n]["ones_made"], 3 * slot + 2)
                    pool.memset(ks[at.kmax:at.kexp, slot, :, :], 1.0).then_inc(S[n]["ones_made"], 1)
                    pool.wait_ge(S[n]["ones_made"], 3 * slot + 3)
                if at.kmax > at.kprod:
                    for n2, t in enumerate((qs, ks)):
                        pool.memset(t[at.kprod:at.kmax, :, :, :], 0.0).then_inc(S[n]["ones_made"], 1)
                        pool.wait_ge(S[n]["ones_made"], 3 * SLOTS + 1 + n2)

            def copy_v(at, g, r):
                dst = vs[:, r % SLOTS, :, :].rearrange("p t (h v) -> p t h v", v=VW)[:, :, :, 0:at.hd]
                src = by_group(vall, at)[:, bass.ds(g, 1), :, :].rearrange("p g i (h d) -> p (g i) h d", h=HG)
                pool.tensor_copy(dst, src).then_inc(S[at.n]["v_copied"], 1)

            for at in ATT:
                s = S[at.n]
                if at.n == 1:
                    pool.wait_ge(S[0]["pv_done"], NS * ATT[0].groups)
                pads(at, at.n)
                if at.n == 1:
                    for m in range(2 * NB):
                        q, low = rope[:, m % 2, 2, :], rest[:, m % 2, :]
                        pool.wait_ge(s["hi"], m + 1)
                        need(pool, s["lo"], m - 1)
                        pool.tensor_tensor(low, q, parts[:, m % 4, 0, :], ALU.subtract).then_inc(s["r1"], 1)
                        pool.wait_ge(s["mid"], m + 1)
                        pool.tensor_tensor(parts[:, m % 4, 2, :], low, parts[:, m % 4, 1, :],
                                           ALU.subtract).then_inc(s["lo"], 1)
                pool.wait_ge(s["v_done"], NB)
                copy_v(at, 0, 0)

                def step(g, r, k, first, last, at=at, s=s):
                    for n, v in enumerate(MASKED):
                        st, h0, nh = UNITS[v]
                        p = pr[:, st % PSLOTS, h0:h0 + nh, 0:P]
                        pool.wait_ge(s["p_ready"], g * NU + v + 1)
                        pool.sem_inc(s["p_seen"])
                        pool.affine_select(out=p, in_=p, compare_op=ALU.is_ge, fill=0.0, base=0,
                                           pattern=[[0, nh], [1, P]], channel_multiplier=-1).then_inc(s["pm_ready"], 1)
                        if n == NM // 2 - 1 and not last:
                            copy_v(at, g + 1, r + 1)

                over_groups(pool, at, step)
                if at.n == 1:
                    for n in range(NB):
                        pool.wait_ge(s["hat_done"], n + 1)
                        t = slice(4 * n, 4 * n + 4)
                        pool.tensor_tensor(x0[:, t, :], x0[:, t, :], x1[:, t, :], ALU.add).then_inc(x12_done, 1)

        @block.tensor
        def _(pe):
            def to_feat(f, tile, ready):
                n = f % NB
                ready(n)
                need(pe, ft_done, f - 1)
                for i in range(4):
                    last = pe.transpose(ps[:, f % 2, i * P:(i + 1) * P], tile(4 * n + i), ident[:, :])
                last.then_inc(ft_ps, 1)

            def project_v(at, src, weight, n):
                s = S[at.n]
                need(pe, s["v_done"], n - 1)
                for i in range(4):
                    last = pe.matmul(ps[:, 2 + n % 2, i * P:(i + 1) * P], src[:, n * 512 + i * P:n * 512 + (i + 1) * P],
                                     weight, start=True, stop=True)
                last.then_inc(s["v_ps"], 1)

            def attention(at):
                s = S[at.n]
                nin = 32 * len(at.products)

                def maxima(u, g, r, k):
                    i, c, h0, nh, w = MAXES[u]
                    bank = ps[:, MAXB + u % 2, :]
                    if u == 0:
                        pe.wait_ge(s["qk_in"][r % SLOTS], (k + 1) * nin)
                    if not (isinstance(g, int) and g == 0 and u < 2):
                        pe.wait_ge(s["mx_free"], g * NX + u - 1)
                    diagonal = 512 * c + w == (i + 1) * P
                    if diagonal:
                        pe.matmul(bank[:, 0:nh * w].rearrange("p (h w) -> p h w", h=nh)[:, :, w - P:w],
                                  identb[:, :], cmask[:, 0:nh, :], start=True, stop=False, skip_group_check=True)
                    for h in range(nh):
                        last = pe.matmul(bank[:, h * w:(h + 1) * w],
                                         qs[0:at.kmax, r % SLOTS, h0 + h, i * P:(i + 1) * P],
                                         ks[0:at.kmax, r % SLOTS, h0 + h, 512 * c:512 * c + w],
                                         start=not diagonal, stop=True, skip_group_check=True)
                    last.then_inc(s["mx_ready"], 1)

                def scores(v, g, r):
                    st, h0, nh = UNITS[v]
                    qb, j, lo, n, _ = STEPS[st]
                    if v == 0:
                        pe.wait_ge(s["rows_in"], g * 48 + 48)
                    if not (isinstance(g, int) and g == 0 and v < 2):
                        pe.wait_ge(s["p_ready"], g * NU + v - 1)
                    to = scores_at(v)
                    for h in range(nh):
                        last = pe.matmul(to[:, h, :], ks[0:at.kexp, r % SLOTS, h0 + h, j * P:(j + 1) * P],
                                         qs[0:at.kexp, r % SLOTS, h0 + h, qb * 512 + lo:qb * 512 + lo + n],
                                         start=True, stop=True)
                    last.then_inc(s["st_ready"], 1)

                def weigh(st, g, r):
                    qb, j, lo, n, diagonal = STEPS[st]
                    if st == 0:
                        pe.wait_ge(s["v_copied"], g + 1)
                    if j == 4 * qb and not (isinstance(g, int) and g == 0 and qb == 0):
                        pe.wait_ge(s["ev_ready"], g * 2 + qb)
                    pe.wait_ge(s["p_ready"], g * NU + LAST_UNIT[st] + 1)
                    if diagonal:
                        masks = sum(v <= LAST_UNIT[st] for v in MASKED)
                        pe.wait_ge(s["pm_ready"], g * NM + masks)
                    for h in range(HG):
                        last = pe.matmul(ps[VW * h:VW * (h + 1), PVB, lo:lo + n],
                                         vs[:, r % SLOTS, j, VW * h:VW * (h + 1)], pr[:, st % PSLOTS, h, 0:n],
                                         start=(j == 4 * qb), stop=(st == END[qb]), skip_group_check=True)
                    last.then_inc(s["pv_done"], 1)

                def turn(q, g, index):
                    pe.wait_ge(s["ev_ready"], g * 2 + q + 1)
                    pe.wait_ge(s["tp_free"], index)
                    for t in range(4):
                        last = pe.transpose(ps[:, TURNB, t * P:(t + 1) * P], ot[:, q, t * P:(t + 1) * P], ident[:, :])
                    last.then_inc(s["tp_ready"], 1)

                def turn_max(g, r, index):
                    pe.wait_ge(s["nm_ready"], g + 1)
                    need(pe, s["tp_free"], index)
                    pe.transpose(ps[0:HG * TB, TURNB, 0:P], nmax[:, r % SLOTS, :], ident[:, :]).then_inc(s["tp_ready"], 1)

                def step(g, r, k, first, last):
                    for what, i, dg in events(first, last):
                        if what == "scores":
                            scores(i, g, r)
                        elif what == "max":
                            maxima(i, g + 1, r + 1, k + 1 if (r + 1) % SLOTS == 0 else k)
                        elif what == "pv":
                            weigh(i, g + dg, r + dg)
                        elif what == "turn":
                            turn(i, g + dg, turn_index(what, i, g, dg))
                        else:
                            turn_max(g + 1, r + 1, turn_index(what, i, g, dg))

                pe.wait_ge(s["ones_made"], 3 * SLOTS + 2 * (at.kmax > at.kprod))
                for u in range(NX):
                    maxima(u, 0, 0, 0)
                turn_max(0, 0, 0)
                over_groups(pe, at, step)

            def att_tile(t):
                return att[:, t % TB, (t // TB) * C:(t // TB + 1) * C]

            def output(at, weight, f):
                s = S[at.n]
                pe.wait_ge(s["at_done"], 2 * at.groups)
                for n in range(NB + 1):
                    if n < NB:
                        to_feat(f + n, att_tile, lambda n: None)
                    if n >= 1:
                        m = n - 1
                        pe.wait_ge(ft_done, f + m + 1)
                        need(pe, s["y_done"], m - 1)
                        for i in range(4):
                            last = pe.matmul(ps[:, 2 + m % 2, i * P:(i + 1) * P],
                                             feat[:, m * 512 + i * P:m * 512 + (i + 1) * P], weight, start=True, stop=True)
                        last.then_inc(s["y_ps"], 1)

            pe.wait_ge(made, 3)
            s = S[0]
            for n in range(NB):
                to_feat(n, lambda t: x0[:, t, :], lambda n: pe.wait_ge(x_in[n], 16))
            pe.wait_ge(wqkv_in, 16)
            for m in range(2 * NB):
                n = m % NB
                if m == NB:
                    pe.wait_ge(wk_made, 1)
                if m < NB:
                    pe.wait_ge(ft_done, n + 1)
                need(pe, s["r1"], m - 1)
                pe.matmul(ps[:, 4 + m % 2, :], w_qkv[:, 0:C] if m < NB else wk[:, :],
                          feat[:, n * 512:(n + 1) * 512], start=True, stop=True).then_inc(s["proj"], 1)
            for n in range(NB):
                project_v(ATT[0], feat, w_qkv[:, 2 * C:3 * C], n)
            attention(ATT[0])
            pe.wait_ge(w_in, 16 * 12)
            output(ATT[0], w_out[:, :], NB)

            s = S[1]
            for n in range(NB):
                to_feat(2 * NB + n, lambda t: xn[:, t, :], lambda n: pe.wait_ge(S[0]["hat_done"], n + 1))
            for t in range(NT):
                if t % 4 == 0:
                    pe.wait_ge(ft_done, 2 * NB + t // 4 + 1)
                last = pe.matmul(ps[:, 2 + t // TB, (t % TB) * LAT:(t % TB + 1) * LAT], feat[:, t * P:(t + 1) * P],
                                 wdkv[:, :], start=True, stop=True)
                if t % TB == TB - 1:
                    last.then_inc(lat_ps, 1)

            def project2(m):
                n = m % NB
                need(pe, s["rope_t"], m - 1)
                for half in range(2):
                    if m < NB:
                        last = pe.matmul(ps[:, 4 + 2 * half + m % 2, :], wq2[:, half, :],
                                         feat[:, n * 512:(n + 1) * 512], start=True, stop=True)
                    else:
                        last = pe.matmul(ps[:, 4 + 2 * half + m % 2, :], wuk[:, half, :],
                                         latT[:, n * 512:(n + 1) * 512], start=True, stop=True)
                last.then_inc(s["proj"], 1)

            pe.wait_ge(wr_made, 4)
            for m in range(NB):
                project2(m)
            for n in range(NB):
                pe.wait_ge(lat_done, n + 1)
                need(pe, latt_done, n - 1)
                for i in range(4):
                    last = pe.transpose(ps[0:LAT, n % 2, i * P:(i + 1) * P], lat[:, 4 * n + i, :], ident[:, :])
                last.then_inc(latt_ps, 1)
            for m in range(NB, 2 * NB):
                pe.wait_ge(latt_done, m - NB + 1)
                project2(m)
            for n in range(NB):
                project_v(ATT[1], latT, wuv[:, :], n)
            attention(ATT[1])
            output(ATT[1], wo[:, :], 3 * NB)

            for n in range(NB):
                to_feat(4 * NB + n, lambda t: xn[:, t, :], lambda n: pe.wait_ge(S[1]["hat_done"], n + 1))
            for t in range(NT):
                if t % 4 == 0:
                    pe.wait_ge(ft_done, 4 * NB + t // 4 + 1)
                last = pe.matmul(ps[:, 2, t * E:(t + 1) * E], feat[:, t * P:(t + 1) * P], gate_w[:, :],
                                 start=True, stop=True)
            last.then_inc(gl_ps, 1)
            pe.wait_ge(moe_in, 16 * 6)
            pe.wait_ge(gl_read, 1)

            def experts(n):
                for c in range(E * HC + 2):
                    if c < E * HC:
                        if not (isinstance(n, int) and n == 0 and c < 4):
                            pe.wait_ge(h_dve if c % 2 else h_act, n * (E * HC // 2) + (c - 4) // 2 + 1)
                        pe.matmul(ps[:, c % 4, :], w1[:, c * P:(c + 1) * P], feat[:, bass.ds(n * 512, 512)],
                                  start=True, stop=True).then_inc(h_ps, 1)
                    if c >= 2:
                        c -= 2
                        if c == 0:
                            if not (isinstance(n, int) and n == 0):
                                pe.wait_ge(y2_free, n * 4)
                            for t in range(4):
                                pe.matmul(ps[:, 4 + t, :], ones3[0:3, :], b2p[0:3, :], start=True, stop=False,
                                          skip_group_check=True)
                        pe.wait_ge(h_dve if c % 2 else h_act, n * (E * HC // 2) + c // 2 + 1)
                        for t in range(4):
                            last = pe.matmul(ps[:, 4 + t, (c // HC) * C:(c // HC + 1) * C],
                                             hid[:, c // 4, c % 4, t * P:(t + 1) * P], w2[:, c, :],
                                             start=False, stop=(c == E * HC - 1), skip_group_check=True)
                last.then_inc(y2_ps, 1)

            experts(0)
            with pe.Fori(1, NB) as n:
                experts(n)

        @block.scalar
        def _(act):
            def from_bank(f, scale=None):
                act.wait_ge(ft_ps, f + 1)
                dst, src = feat[:, (f % NB) * 512:(f % NB + 1) * 512], ps[:, f % 2, :]
                if scale is None:
                    act.copy(dst, src).then_inc(ft_done, 1)
                else:
                    act.activation(dst, src, ACT.Identity, scale=scale).then_inc(ft_done, 1)

            def split(at, source, ready):
                s = S[at.n]
                for m in range(2 * NB + 1):
                    if m < 2 * NB:
                        act.wait_ge(s[ready], m + 1)
                        if m >= 4:
                            act.wait_ge(s["stored"][m % 4], 16)
                        act.copy(parts[:, m % 4, 0, :], source(m)).then_inc(s["hi"], 1)
                    if m >= 1:
                        act.wait_ge(s["r1"], m)
                        act.copy(parts[:, (m - 1) % 4, 1, :], rest[:, (m - 1) % 2, :]).then_inc(s["mid"], 1)

            def attention(at):
                s = S[at.n]

                def copy_out(q, g):
                    act.wait_ge(s["pv_done"], g * NS + END[q] + 1)
                    act.copy(ot[:, q, :], ps[:, PVB, :]).then_inc(s["ev_ready"], 1)

                def step(g, r, k, first, last):
                    for st in range(NS):
                        n = STEPS[st][3]
                        for v in range(FIRST_UNIT[st], LAST_UNIT[st] + 1):
                            _, h0, nh = UNITS[v]
                            if v == FIRST_UNIT[st] and not (isinstance(g, int) and g == 0 and st < PSLOTS):
                                act.wait_ge(s["pv_done"], g * NS + st - PSLOTS + 1)
                            act.wait_ge(s["st_ready"], g * NU + v + 1)
                            act.activation(pr[:, st % PSLOTS, h0:h0 + nh, 0:n], scores_at(v), ACT.Exp,
                                           scale=at.scale).then_inc(s["p_ready"], 1)
                        if st == LAG - 1 and not first:
                            copy_out(1, g - 1)
                        if st == END[0] + LAG:
                            copy_out(0, g)
                    if last:
                        copy_out(1, g)

                over_groups(act, at, step)

            def root(n, eps, src, dst, scale=1.0):
                act.activation(dst, src, ACT.Sqrt, bias=eps[:, 0:1], scale=scale).then_inc(root_done[n], 1)

            def rms(at):
                s, x = S[at.n], (x1, x0)[at.n]
                for n in range(NB):
                    act.wait_ge(s["ssq_in"], n + 1)
                    act.activation(feat[:, n * 512:(n + 1) * 512].rearrange("p (t c) -> p t c", c=C),
                                   x[:, 4 * n:4 * n + 4, :], ACT.Square).then_inc(s["ssq_out"], 1)
                act.wait_ge(s["ss_ready"], 1)
                act.activation(rstd[:, 2, :], rstd[:, 3, :], ACT.Sqrt, bias=eps6[:, 0:1],
                               scale=1.0 / C).then_inc(s["rms_sq"], 1)

            for f in range(NB):
                from_bank(f)
            split(ATT[0], lambda m: ps[:, 4 + m % 2, :], "proj")
            attention(ATT[0])
            for f in range(NB, 2 * NB):
                from_bank(f)
            act.wait_ge(made, 7)
            act.wait_ge(var_ready[0], 1)
            root(0, eps5, mv[:, :, 1], rstd[:, 0, :])
            rms(ATT[0])
            act.wait_ge(w_in, 16 * 12)
            for f in range(2 * NB, 3 * NB):
                from_bank(f, norm_w[:, 0:1])
            act.wait_ge(var_ready[1], 1)
            root(1, eps5, mv[:, :, 1], rstd[:, 0, :])
            s = S[1]

            def hi(m):
                act.wait_ge(s["rope_q"], m + 1)
                if m >= 4:
                    act.wait_ge(s["stored"][m % 4], 16)
                act.copy(parts[:, m % 4, 0, :], rope[:, m % 2, 2, :]).then_inc(s["hi"], 1)

            def mid(m):
                act.wait_ge(s["r1"], m + 1)
                act.copy(parts[:, m % 4, 1, :], rest[:, m % 2, :]).then_inc(s["mid"], 1)

            for m in range(NB):
                hi(m)
                mid(m)
            for n in range(NB):
                act.wait_ge(latt_ps, n + 1)
                act.activation(latT[:, n * 512:(n + 1) * 512], ps[0:LAT, n % 2, :], ACT.Identity,
                               scale=ln_gb[:, 0:1], bias=ln_gb[:, 1:2]).then_inc(latt_done, 1)
            for m in range(NB, 2 * NB):
                hi(m)
                mid(m)
            attention(ATT[1])
            for f in range(3 * NB, 4 * NB):
                from_bank(f)
            rms(ATT[1])
            for f in range(4 * NB, 5 * NB):
                from_bank(f, norm_w[:, 1:2])

            def experts(n):
                for c in range(0, E * HC, 2):
                    act.wait_ge(h_ps, n * (E * HC) + c + 1)
                    act.activation(hid[:, c // 4, c % 4, :], ps[:, c % 4, :], ACT.Relu,
                                   bias=b1[:, c:c + 1]).then_inc(h_act, 1)

            act.wait_ge(moe_in, 16 * 6)
            experts(0)
            with act.Fori(1, NB) as n:
                experts(n)
            act.wait_ge(var_ready[2], 1)
            root(2, eps5, mv[:, :, 1], rstd[:, 0, :])

        @block.vector
        def _(dve):
            linked = [0]

            def link(ins):
                linked[0] += 1
                ins.then_inc(dchain, 1)
                dve.wait_ge(dchain, linked[0])

            def attention(at):
                s = S[at.n]

                def reduce(u, g, r):
                    i, c, h0, nh, w = MAXES[u]
                    dve.wait_ge(s["mx_ready"], g * NX + u + 1)
                    dve.tensor_reduce(mparts[:, r % SLOTS, h0:h0 + nh, i, c],
                                      ps[:, MAXB + u % 2, 0:nh * w].rearrange("p (h w) -> p h w", h=nh),
                                      AX_X, ALU.max).then_inc(s["mx_free"], 1)

                def combine(g, r):
                    dve.wait_ge(s["mx_free"], g * NX + NX)
                    dve.tensor_reduce(nmax[:, r % SLOTS, :], mparts[:, r % SLOTS, :, :, :].rearrange("p h i c -> p (h i) c"),
                                      AX_X, ALU.max, negate=True).then_inc(s["nm_ready"], 1)

                def split_max(g, r, index):
                    src, np = ps[0:HG * TB, TURNB, 0:P], nparts[:, r % SLOTS, :, :]
                    dve.wait_ge(s["tp_ready"], index + 1)
                    dve.tensor_copy(np[:, 0, :], src).then_inc(s["ns_hi"], 1)
                    dve.wait_ge(s["ns_hi"], g + 1)
                    dve.tensor_tensor(nrow[:, 0, :], src, np[:, 0, :], ALU.subtract).then_inc(s["tp_free"], 1)
                    dve.wait_ge(s["tp_free"], index + 1)
                    dve.tensor_copy(np[:, 1, :], nrow[:, 0, :]).then_inc(s["ns_mid"], 1)
                    dve.wait_ge(s["ns_mid"], g + 1)
                    dve.tensor_tensor(np[:, 2, :], nrow[:, 0, :], np[:, 1, :], ALU.subtract).then_inc(s["np_ready"], 1)

                def normalise(q, g, index):
                    src = turned(at)
                    dve.wait_ge(s["tp_ready"], index + 1)
                    dve.reciprocal(rc[:, q, :, :], src[:, :, :, at.hd]).then_inc(s["rc_done"], 1)
                    dve.wait_ge(s["rc_done"], g * 2 + q + 1)
                    dst = att[:, 4 * q:4 * q + 4, bass.ds(g * at.gw, at.gw)].rearrange("p i (h d) -> p i h d", h=HG)
                    w = rc[:, q, :, :].unsqueeze(3).broadcast_to([P, 4, HG, at.hd])
                    dve.tensor_tensor(dst, src[:, :, :, 0:at.hd], w, ALU.mult).then_inc(s["tp_free"], 1)
                    if q == 1:
                        pass

                def step(g, r, k, first, last):
                    waiting, since = None, 0
                    for what, i, dg in events(first, last):
                        if what == "max":
                            reduce(i, g + 1, r + 1)
                            since += 1
                            if i == NX - 1:
                                combine(g + 1, r + 1)
                        if waiting and (since >= 2 or what == "turnmax"):
                            normalise(*waiting)
                            waiting = None
                        if what == "turn":
                            waiting, since = (i, g + dg, turn_index(what, i, g, dg)), 2 if last else 0
                            if last:
                                normalise(*waiting)
                                waiting = None
                        elif what == "turnmax":
                            split_max(g + 1, r + 1, turn_index(what, i, g, dg))
                    assert waiting is None

                dve.wait_ge(made, 7)
                for u in range(NX):
                    reduce(u, 0, 0)
                combine(0, 0)
                split_max(0, 0, 0)
                over_groups(dve, at, step)
                dve.wait_ge(s["tp_free"], 3 * at.groups)
                dve.engine_nop().then_inc(s["at_done"], 2 * at.groups)

            def residual(at, n, x, to):
                s = S[at.n]
                dve.wait_ge(s["y_ps"], n + 1)
                t = slice(4 * n, 4 * n + 4)
                dve.tensor_tensor(to[:, t, :], x[:, t, :], ps[:, 2 + n % 2, :].rearrange("p (t c) -> p t c", c=C),
                                  ALU.add).then_inc(s["y_done"], 1)
                dve.wait_ge(s["y_done"], n + 1)

            def moments(src, tiles):
                for t in tiles:
                    last = dve.bn_stats(stats[:, t, :], src(t))
                link(last)
                for t in tiles:
                    last = dve.bn_aggr(mv[:, t, :], stats[:, t, :])
                return last

            def rms(at, x):
                s = S[at.n]
                for n in range(NB):
                    dve.wait_ge(s["ssq_out"], n + 1)
                    last = dve.tensor_reduce(rstd[:, 3, 4 * n:4 * n + 4],
                                             feat[:, n * 512:(n + 1) * 512].rearrange("p (t c) -> p t c", c=C), AX_X, ALU.add)
                last.then_inc(s["ss_ready"], 1)
                dve.wait_ge(s["rms_sq"], 1)
                link(dve.reciprocal(rstd[:, 1, :], rstd[:, 2, :]))
                for t in range(NT):
                    last = dve.tensor_scalar(xn[:, t, :], x[:, t, :], rstd[:, 1, t:t + 1], None, ALU.mult)
                    if t % 4 == 3:
                        last.then_inc(s["hat_done"], 1)

            def v_out(at):
                s = S[at.n]
                for n in range(NB):
                    dve.wait_ge(s["v_ps"], n + 1)
                    b = n // 2
                    dst = by_group(vall, at)[:, b * at.gb:(b + 1) * at.gb, (n % 2) * 4:(n % 2) * 4 + 4, :]
                    dve.tensor_copy(dst, ps[:, 2 + n % 2, :].rearrange("p (i g w) -> p g i w", i=4, g=at.gb)).then_inc(s["v_done"], 1)

            dve.wait_ge(wqkv_in, 16)
            dve.wait_ge(geo_in, 32)
            first3 = w_qkv[:, C:2 * C].rearrange("p (h d) -> p h d", h=8)[:, :, 0:3]
            link(dve.tensor_copy(wk[:, :], w_qkv[:, C:2 * C]))
            link(dve.tensor_tensor(geo[:, :, :], first3, sign[:, :, :], ALU.mult))
            link(dve.tensor_reduce(geot[:, :], geo[:, :, :], AX_X, ALU.add))
            link(dve.tensor_tensor(geou[:, :], geot[:, :], hs[:, :], ALU.mult))
            link(dve.tensor_scalar(geot[:, :], geou[:, :], 1.0 / (3.0 * ATT[0].scale), None, ALU.mult))
            link(dve.tensor_tensor(geo[:, :, :], sign[:, :, :], geot[:, :].unsqueeze(2).broadcast_to([P, 8, 3]), ALU.mult))
            wk3 = wk[:, :].rearrange("p (h d) -> p h d", h=8)[:, :, 0:3]
            dve.tensor_tensor(wk3, first3, geo[:, :, :], ALU.add).then_inc(wk_made, 1)

            s = S[0]
            for m in range(2 * NB + 1):
                if m < 2 * NB:
                    dve.wait_ge(s["hi"], m + 1)
                    need(dve, s["lo"], m - 1)
                    dve.tensor_tensor(rest[:, m % 2, :], ps[:, 4 + m % 2, :], parts[:, m % 4, 0, :],
                                      ALU.subtract).then_inc(s["r1"], 1)
                if m >= 1:
                    m -= 1
                    dve.wait_ge(s["mid"], m + 1)
                    dve.tensor_tensor(parts[:, m % 4, 2, :], rest[:, m % 2, :], parts[:, m % 4, 1, :],
                                      ALU.subtract).then_inc(s["lo"], 1)
            v_out(ATT[0])
            dve.wait_ge(b2_in, 16)
            dve.tensor_copy(b2s[:, 0, :], b2[:, :]).then_inc(b2_split, 1)
            dve.wait_ge(b2_split, 1)
            link(dve.tensor_tensor(b2r[:, :], b2[:, :], b2s[:, 0, :], ALU.subtract))
            dve.tensor_copy(b2s[:, 1, :], b2r[:, :]).then_inc(b2_split, 1)
            dve.wait_ge(b2_split, 2)
            dve.tensor_tensor(b2s[:, 2, :], b2r[:, :], b2s[:, 1, :], ALU.subtract).then_inc(b2_split, 1)
            dve.wait_ge(w_in, 16 * 12)
            half = ATT[1].hd // 2
            for w in (wq2, wuk):
                own = w[:, 0, :].rearrange("p (h d) -> p h d", d=2 * half)
                pair = w[:, 1, :].rearrange("p (h d) -> p h d", d=2 * half)
                dve.tensor_scalar(pair[:, :, 0:half], own[:, :, half:2 * half], -1.0, None, ALU.mult).then_inc(wr_made, 1)
                dve.tensor_copy(pair[:, :, half:2 * half], own[:, :, 0:half]).then_inc(wr_made, 1)
            attention(ATT[0])

            for n in range(NB):
                residual(ATT[0], n, x0, xn)
                last = moments(lambda t: xn[:, t, :], range(4 * n, 4 * n + 4))
            last.then_inc(var_ready[0], 1)
            dve.wait_ge(root_done[0], 1)
            link(dve.reciprocal(rstd[:, 1, :], rstd[:, 0, :]))
            for t in range(NT):
                last = dve.tensor_scalar(x1[:, t, :], xn[:, t, :], mv[:, t, 0:1], rstd[:, 1, t:t + 1],
                                         ALU.subtract, ALU.mult)
                if t % 4 == 3:
                    last.then_inc(S[0]["ssq_in"], 1)
            rms(ATT[0], x1)

            s = S[1]

            def latent(t):
                return ps[:, 2 + t // TB, (t % TB) * LAT:(t % TB + 1) * LAT]

            def rotate(m):
                at = slice((m % 2) * 512, (m % 2) * 512 + 512)
                dve.wait_ge(s["proj"], m + 1)
                need(dve, s["r1"], m - 1)
                dve.tensor_tensor(rope[:, m % 2, 0, :], ps[:, 4 + m % 2, :], cos[:, at], ALU.mult)
                dve.tensor_tensor(rope[:, m % 2, 1, :], ps[:, 6 + m % 2, :], sin[:, at], ALU.mult).then_inc(s["rope_t"], 1)
                dve.wait_ge(s["rope_t"], m + 1)
                dve.tensor_tensor(rope[:, m % 2, 2, :], rope[:, m % 2, 0, :], rope[:, m % 2, 1, :],
                                  ALU.add).then_inc(s["rope_q"], 1)

            for b in range(2):
                dve.wait_ge(lat_ps, b + 1)
                last = moments(latent, range(b * TB, (b + 1) * TB))
            last.then_inc(var_ready[1], 1)
            dve.wait_ge(cs_in, 32)
            rotate(0)
            dve.wait_ge(root_done[1], 1)
            link(dve.reciprocal(rstd[:, 1, :], rstd[:, 0, :]))
            for t in range(NT):
                last = dve.tensor_scalar(lat[:, t, :], latent(t), mv[:, t, 0:1], rstd[:, 1, t:t + 1],
                                         ALU.subtract, ALU.mult)
                if t % 4 == 3:
                    last.then_inc(lat_done, 1)
            for m in range(1, 2 * NB):
                rotate(m)
            v_out(ATT[1])
            attention(ATT[1])

            for n in range(NB):
                residual(ATT[1], n, x1, x0)
                dve.engine_nop().then_inc(S[1]["ssq_in"], 1)
            rms(ATT[1], x0)

            dve.wait_ge(gl_ps, 1)
            gates = ps[:, 2, 0:NT * E].rearrange("p (t e) -> p t e", e=E)
            dve.tensor_tensor(logit[:, :, :], gates, gate_b[:, :].unsqueeze(1).broadcast_to([P, NT, E]), ALU.add).then_inc(gl_read, 1)
            dve.wait_ge(gl_read, 1)
            link(dve.tensor_reduce(lmax[:, :], logit[:, :, :], AX_X, ALU.max))
            link(dve.tensor_tensor(eq[:, :, :], logit[:, :, :], lmax[:, :].unsqueeze(2).broadcast_to([P, NT, E]), ALU.is_equal))
            dve.tensor_copy(onehot[:, :, 0], eq[:, :, 0])
            for e in range(1, E):
                before = eq[:, :, 0] if e == 1 else used[:, e % 2, :]
                link(dve.tensor_tensor(onehot[:, :, e], eq[:, :, e], before, ALU.is_gt))
                if e < E - 1:
                    link(dve.tensor_tensor(used[:, (e + 1) % 2, :], before, eq[:, :, e], ALU.max))
            dve.wait_ge(moe_in, 16 * 6)
            dve.wait_ge(x12_done, NB)

            def experts(n):
                for c in range(1, E * HC, 2):
                    dve.wait_ge(h_ps, n * (E * HC) + c + 1)
                    dve.tensor_scalar(hid[:, c // 4, c % 4, :], ps[:, c % 4, :], b1[:, c:c + 1], 0.0,
                                      ALU.add, ALU.max).then_inc(h_dve, 1)
                dve.wait_ge(y2_ps, n + 1)
                for e in range(E):
                    if e:
                        dve.wait_ge(y2_acc, n * 12 + 4 * e)
                    for t in range(4):
                        to = xn[:, bass.ds(n * 4 + t, 1), :].rearrange("p t c -> p (t c)")
                        x12 = x0[:, bass.ds(n * 4 + t, 1), :].rearrange("p t c -> p (t c)")
                        pick = onehot[:, bass.ds(n * 4 + t, 1), e]
                        dve.scalar_tensor_tensor(out=to, in0=ps[:, 4 + t, e * C:(e + 1) * C], scalar=pick,
                                                 in1=x12 if e == 0 else to, op0=ALU.mult,
                                                 op1=ALU.add).then_inc(y2_acc if e < E - 1 else y2_free, 1)

            experts(0)
            with dve.Fori(1, NB) as n:
                experts(n)

            dve.wait_ge(y2_free, 4 * NB)
            last = moments(lambda t: xn[:, t, :], range(NT))
            last.then_inc(var_ready[2], 1)
            dve.wait_ge(root_done[2], 1)
            link(dve.reciprocal(rstd[:, 1, :], rstd[:, 0, :]))
            for t in range(NT):
                last = dve.tensor_scalar(xn[:, t, :], xn[:, t, :], mv[:, t, 0:1], rstd[:, 1, t:t + 1],
                                         ALU.subtract, ALU.mult)
                if t % 4 == 3:
                    last.then_inc(fin_done, 1)


OUT = ((B, T, C), "float32")


def shape_constants():
    half = ATT[1].hd // 2
    inv = (np.float32(1.0) / np.power(np.float32(10000.0), np.arange(half, dtype=np.float32) / np.float32(half))).astype(np.float32)
    angle = (np.arange(T, dtype=np.float32)[None, :] * inv[:, None]).astype(np.float32)
    angle = np.tile(angle, (C // half, 1))
    signs = np.array([[(i >> 2 & 1) * 2 - 1, (i >> 1 & 1) * 2 - 1, (i & 1) * 2 - 1] for i in range(8)], np.float32)
    return {"cos": np.cos(angle), "sin": np.sin(angle), "sign": np.tile(signs.reshape(1, 24), (P, 1))}


def kernel(L0_attn_x, L0_attn_w_qkv, L0_attn_w_out, L0_attn_head_scales, L0_ffn_norm1_w, L0_ffn_norm2_w,
           L0_ffn_Wq, L0_ffn_Wdkv, L0_ffn_Wuk, L0_ffn_Wuv, L0_ffn_Wo, L0_ffn_ln_g, L0_ffn_ln_b,
           L0_ffn_gate_w, L0_ffn_gate_b, L0_ffn_W1, L0_ffn_b1, L0_ffn_W2, L0_ffn_b2):
    import concourse.bacc as bacc
    from concourse.bass_utils import run_bass_kernel_spmd

    given = {
        "x": L0_attn_x, "w_qkv": L0_attn_w_qkv, "w_out": L0_attn_w_out,
        "hs": np.broadcast_to(np.asarray(L0_attn_head_scales)[None, :], (P, 8)),
        "norm1": np.asarray(L0_ffn_norm1_w)[:, None], "norm2": np.asarray(L0_ffn_norm2_w)[:, None],
        "WqT": np.asarray(L0_ffn_Wq).T, "WdkvT": np.asarray(L0_ffn_Wdkv).T, "WukT": np.asarray(L0_ffn_Wuk).T,
        "WuvT": np.asarray(L0_ffn_Wuv).T, "WoT": np.asarray(L0_ffn_Wo).T,
        "ln_g": np.asarray(L0_ffn_ln_g)[:, None], "ln_b": np.asarray(L0_ffn_ln_b)[:, None],
        "gateT": np.asarray(L0_ffn_gate_w).T, "gate_b": np.broadcast_to(np.asarray(L0_ffn_gate_b)[None, :], (P, E)),
        "W1T": np.asarray(L0_ffn_W1).reshape(E * HID, C).T, "b1T": np.asarray(L0_ffn_b1).reshape(E * HC, P).T,
        "W2T": np.asarray(L0_ffn_W2).transpose(0, 2, 1).reshape(E * HC, P, C).transpose(1, 0, 2),
        "b2": np.asarray(L0_ffn_b2).reshape(1, E * C),
    } | shape_constants()
    nc = bacc.Bacc("TRN2", target_bir_lowering=False, num_devices=1)
    arrays, aps = {}, {}
    for name, value in given.items():
        v = np.ascontiguousarray(value)
        arrays[f"in_{name}"] = v
        aps[name] = nc.dram_tensor(f"in_{name}", v.shape, mybir.dt.from_np(v.dtype), kind="ExternalInput").ap()
    out = nc.dram_tensor("out_0", OUT[0], F32, kind="ExternalOutput").ap()
    build(nc, aps, out)
    r = run_bass_kernel_spmd(nc, [arrays], core_ids=[0])
    return r.results[0]["out_0"]
```

```python
from contextlib import ExitStack

import numpy as np

import concourse.bass as bass
from concourse import mybir

F32 = mybir.dt.float32
BF16 = mybir.dt.bfloat16
I32 = mybir.dt.int32
ALU = mybir.AluOpType
ACT = mybir.ActivationFunctionType
AX_X = mybir.AxisListType.X

P = 128
B, T, C = 2, 1024, 128
NT = B * T // P
TB = T // P
NB = B * T // 512
HG = 4
VW = 32
E, HID = 4, 512
HC = HID // P
LAT = 64
SLOTS = 3
VSLOTS = 2
PSLOTS = 4
PARTS = 3
NEG = -1.0e30


class Attention:

    def __init__(self, n, hd, products, scale):
        self.n, self.hd, self.products, self.scale = n, hd, products, scale
        self.heads = C // hd
        self.gb = self.heads // HG
        self.groups = B * self.gb
        self.gw = HG * hd
        self.kprod = len(products) * hd


ATT = [Attention(0, 16, [(0, 0), (0, 1), (1, 0), (1, 1), (0, 2), (2, 0)], 16 ** -0.5),
       Attention(1, 8, [(0, 0), (0, 1), (1, 0), (1, 1), (0, 2), (2, 0), (1, 2), (2, 1)], 8 ** -0.5)]
KMAX = 96
KEXP = KMAX + 3
GROUPS = [(at, g) for at in ATT for g in range(at.groups)]
NF = len(GROUPS)


def exp_steps():
    out = []
    for qb in range(T // 512):
        for j in [*range(4 * qb, 4 * qb + 4), *range(4 * qb)]:
            lo = max(0, (j - 4 * qb) * P)
            out.append((qb, j, lo, 512 - lo, j >= 4 * qb))
    return out


STEPS = exp_steps()
NS = len(STEPS)
END = [max(s for s in range(NS) if STEPS[s][0] == qb) for qb in range(T // 512)]


def exp_units():
    out = []
    for s, (_, _, _, n, _) in enumerate(STEPS):
        nh = min(HG, 512 // n)
        out += [(s, h, nh) for h in range(0, HG, nh)]
    return out


UNITS = exp_units()
NU = len(UNITS)
LAST_UNIT = [max(v for v in range(NU) if UNITS[v][0] == s) for s in range(NS)]
MASKED = [s for s in range(NS) if STEPS[s][4]]
NM = len(MASKED)


def max_units():
    out = []
    for i in range(TB):
        for c in range(i // 4 + 1):
            w = min(512, (i + 1) * P - 512 * c)
            nh = min(HG, 512 // w)
            out += [(i, c, h, nh, w) for h in range(0, HG, nh)]
    return out


MAXES = max_units()
NX = len(MAXES)
assert NX % 2 == 0 and NS % PSLOTS == 0
LAG = 2

SCB, SCN = 0, 2
SIDEB, PVB = 3, 4
MAXB, MAXN = 5, 3


def split_block(M):
    return M // 8, M // 4 % 2, M // 2 % 2, M % 2


def backbone():
    out = []
    for u in range(NX):
        out.append((-1 + u / (NX + 6), ("max", 0, u)))
    out += [(-0.1, ("combine", 0)), (-0.09, ("turnmax", 0)), (-0.08, ("rows", 0))]
    taken = [NX] + [0] * NF
    later = []
    total = HG * sum(st[3] for st in STEPS)

    for F in range(NF + 1):
        passed = 0

        def add(step, w=0):
            nonlocal passed
            pos = F + passed / total
            out.append((pos, step))
            passed += w
            for e in later:
                e[0] -= 1
            while later and later[0][0] <= 0:
                out.append((pos, later.pop(0)[1]))
            for G in range(F + 1, min(F + 3, NF)):
                lo, hi = MAX_LATE if G == ATT[0].groups else MAX_SPREAD
                while taken[G - 1] == NX and taken[G] < min(NX, int(NX * (F + passed / total - (G - 1) - lo) / (hi - lo))):
                    out.append((pos, ("max", G, taken[G])))
                    taken[G] += 1
                    if taken[G] == NX:
                        out.append((pos, ("combine", G)))
                        for wait, what in ((2, "turnmax"), (2, "rows")):
                            later.append([wait, (what, G)])
                        later.sort(key=lambda e: e[0])

        def product(s):
            if s >= LAG or F:
                G, r = (F, s - LAG) if s >= LAG else (F - 1, s - LAG + NS)
                add(("pv", G, r))
                if r in END:
                    q = END.index(r)
                    for wait, what in ((1, "evac"), (3, "turn")):
                        later.append([wait, (what, G, q)])
                    later.sort(key=lambda e: e[0])

        for s in range(NS if F < NF else LAG):
            units = [v for v in range(NU) if UNITS[v][0] == s] if F < NF else []
            for v in units:
                add(("scores", F, v), UNITS[v][2] * STEPS[s][3])
                if v == units[min(1, len(units) - 1)]:
                    product(s)
            if not units:
                product(s)
            elif STEPS[s][4]:
                out.append((out[-1][0], ("mask", F, s)))
    out += [(NF + 0.5, e[1]) for e in later]
    return out


MAX_SPREAD = (-0.2, 0.78)
MAX_LATE = (0.48, 0.88)


def before_first(b):
    out = [("feed", "x", b, 0), ("feat", "x", b, 0), ("feed", "x", b, 1), ("feat", "x", b, 1)]
    M0 = 4 * b
    for m in range(M0, M0 + 5):
        if m < M0 + 4:
            out.append(("proj", m, 0))
        if m > M0:
            out.append(("mid", m - 1))
        if m < M0 + 4:
            out.append(("hi", m))
        if m > M0:
            out += [("lo", m - 1), ("store", m - 1)]
        if m < M0 + 4:
            out.append(("r1", m))
    for i in range(2):
        out += [("v_proj", 0, b, i), ("v_out", 0, b, i)]
    return out


def rms(n, b):
    out = [("square", n, b, 0), ("square", n, b, 1), ("square_sum", n, b, 0), ("square_sum", n, b, 1),
           ("rms_rec", n, b), ("hat", n, b, 0), ("hat", n, b, 1)]
    for i in range(2):
        if n:
            out.append(("x12", b, i))
        out += [("feed", f"hat{n}", b, i), ("feat", f"hat{n}", b, i)]
    return out


def output(n, b):
    out = []
    for i in range(2):
        out += [("feed", f"att{n}", b, i), ("feat", f"att{n}", b, i)]
    for i in range(2):
        out += [("y", n, b, i), ("residual", n, b, i)]
    return out


def between(b):
    out = output(0, b) + [("moments", 0, b, 0), ("moments", 0, b, 1), ("layer_norm", 0, b, 0),
                          ("layer_norm", 0, b, 1)] + rms(0, b)
    M0 = 8 + 4 * b
    tail = {}

    def block(m):
        rest = tail.pop(m - 1, [])
        own = [("proj", m, 0), ("rotate", m, 0), ("proj", m, 1), ("rotate", m, 1), ("rotated", m)]
        tail[m] = [("hi", m), ("r1", m), ("mid", m), ("lo", m), ("store", m)]
        mixed = []
        for k in range(5):
            mixed.append(own[k])
            mixed += rest[k:k + 1]
        return mixed

    out += [("latent", b), ("lat_copy", b)]
    q0 = block(M0)
    out += q0[:2] + [("lat_moments", b)] + q0[2:]
    q1 = block(M0 + 1)
    out += q1[:3] + [("lat_norm", b)] + q1[3:]
    for i in range(2):
        out += [("lat_turn", b, i), ("lat_feat", b, i)]
    out += block(M0 + 2) + block(M0 + 3)
    v = []
    for i in range(2):
        v += [("v_proj", 1, b, i), ("v_out", 1, b, i)]
    last = tail.pop(M0 + 3)
    for k in range(5):
        out += [last[k]] + v[k:k + 1]
    return out


def after_second(b):
    out = output(1, b) + rms(1, b) + [("gate", b), ("pick", b)]
    NCH = E * HC
    for c in range(2 * NCH + 2):
        if c < 2 * NCH:
            out += [("hidden", b, c // NCH, c % NCH), ("relu", b, c // NCH, c % NCH)]
        if c % HC == 1 and c > HC:
            e = c // HC - 1
            out += [("expert", b, e // E, e % E), ("pick_up", b, e // E, e % E)]
            if e == E - 1:
                out.append(("moments", 2, b, 0))
    out.append(("moments", 2, b, 1))
    for i in range(2):
        out += [("layer_norm", 2, b, i), ("out", b, i)]
    return out


def spread(steps, first, last):
    return [(first + (last - first) * k / len(steps), s) for k, s in enumerate(steps)]


def schedule():
    late = 3.42
    out = backbone()
    out += spread(before_first(0), -3, -2) + [(-2, ("load", 0)), (-2, ("load", 1))]
    out += spread(before_first(1), -1.99, -1.01) + [(-1.0, ("copy_v", 0))]
    out += [(0.02, ("load", 2)), (0.05, ("weights",)), (0.1, ("partners",)), (0.6, ("b2_parts",)), (1.02, ("load", 3))]
    out += [(-1.005 + 0.7 * F, ("pads", F)) for F in range(SLOTS)]
    out += spread(between(0), 2.3, late) + [(late, ("load", 4)), (late, ("load", 5))]
    out += spread(between(1), 4.3, 5.95)
    out += [(F - 2 + 0.02, ("load", F)) for F in range(6, NF)]
    out += [(F - 1 + 0.4, ("copy_v", F)) for F in range(1, NF)]
    out += [(F - 2 + 0.1, ("zeros", F)) for F in range(ATT[0].groups, ATT[0].groups + SLOTS)]
    out += spread(after_second(0), 8.3, 11.98)
    out += [(12.9, ("quiet",))] + spread(after_second(1), 13, 14)
    return [s for _, s in sorted(out, key=lambda e: e[0])]


SCHEDULE = schedule()
READER = {"feed": "feat", "y": "residual", "latent": "lat_copy", "lat_turn": "lat_feat", "v_proj": "v_out",
          "gate": "pick", "hidden": "relu", "expert": "pick_up"}


def plan():
    nth, bank_of, freed_by, turn_of = {}, {}, {}, {}
    seen, reader = {}, {}
    banks, k = list(range(8)), 0
    for s in SCHEDULE:
        kind = s[0]
        seen[kind] = seen.get(kind, 0) + 1
        assert s not in nth
        nth[s] = seen[kind]
        if kind == "load":
            banks = [2, SIDEB] if s[1] == 2 else ([0, 1, 2, 3] if s[1] == 0 else banks)
        elif kind == "quiet":
            banks = list(range(8))
        if kind in READER or kind == "proj":
            bank = banks[k % len(banks)]
            k += 1
            bank_of[s] = bank
            if bank in reader:
                assert reader[bank] in nth, (s, reader[bank])
                freed_by[s] = reader[bank]
            if kind == "proj":
                reader[bank] = ("r1", s[1]) if s[1] < 8 else ("rotate", s[1], s[2])
            else:
                reader[bank] = (READER[kind],) + s[1:]
        if kind in ("max", "turn", "turnmax"):
            turn_of[s] = len(turn_of) + 1
    return nth, bank_of, freed_by, turn_of


NTH, BANK_OF, FREED_BY, TURN_OF = plan()
STEP_KINDS = sorted({s[0] for s in SCHEDULE})


def nth(*step):
    return NTH[step]


def build(nc, a, out):
    ctx = ExitStack()
    with ctx:
        def sb(name, shape, dt=F32):
            return ctx.enter_context(nc.sbuf_tensor(name, shape, dt))

        def sem(name):
            return ctx.enter_context(nc.semaphore(name))

        ps = ctx.enter_context(nc.psum_tensor("ps", [P, 8, 512], F32))

        ident = sb("ident", [P, P])
        identb = sb("identb", [P, P], BF16)
        cmask = sb("cmask", [P, HG, P], BF16)
        w_qkv = sb("w_qkv", [P, 3 * C])
        w_out = sb("w_out", [P, C])
        hs = sb("hs", [P, 8])
        sign = sb("sign", [P, 8, 3])
        geo = sb("geo", [P, 8, 3])
        geot = sb("geot", [P, 8])
        geou = sb("geou", [P, 8])
        wk = sb("wk", [P, C])
        norm_w = sb("norm_w", [P, 2])
        wq2 = sb("wq2", [P, 2, C])
        wdkv = sb("wdkv", [P, LAT])
        wuk = sb("wuk", [LAT, 2, C])
        wuv = sb("wuv", [LAT, C])
        wo = sb("wo", [P, C])
        ln_gb = sb("ln_gb", [LAT, 2])
        gate_w = sb("gate_w", [P, E])
        gate_b = sb("gate_b", [P, E])
        cos = sb("cos", [P, T])
        sin = sb("sin", [P, T])
        w1 = sb("w1", [P, E * HID])
        b1 = sb("b1", [P, E * HC])
        w2 = sb("w2", [P, E * HC, C])
        b2p = sb("b2p", [3, E * C], BF16)
        ones3 = sb("ones3", [3, P], BF16)

        x0 = sb("x0", [P, NT, C])
        x1 = sb("x1", [P, NT, C])
        xn = sb("xn", [P, NT, C])
        feat = sb("feat", [P, B * T])
        att = sb("att", [P, TB, B * C])
        stats = sb("stats", [P, NT, 6])
        mv = sb("mv", [P, NT, 2])
        rstd = sb("rstd", [P, 5, NT])
        parts = sb("parts", [P, PARTS, 3, 512], BF16)
        vall = sb("vall", [P, B * T])

        work = sb("work", [P, 2 * HC * 512])
        hid = work[:, :].rearrange("p (s c n) -> p s c n", s=2, c=HC)
        rest = work[:, 0:1024].rearrange("p (s n) -> p s n", s=2)
        rope = work[:, 1024:2560].rearrange("p (s n) -> p s n", s=3)
        lat = work[:, 2560:3072].rearrange("p (t l) -> p t l", l=LAT)
        latT = work[0:LAT, 3072:4096]
        b2, b2r = rope[0:1, 0, :], rope[0:1, 1, :]
        b2s = parts[0:1, 2, :, :]

        qs = sb("qs", [P, SLOTS, HG, T], BF16)
        ks = sb("ks", [P, SLOTS, HG, T], BF16)
        vs = sb("vs", [P, VSLOTS, TB, HG * VW])
        pr = sb("pr", [P, PSLOTS, HG, 512])
        ot = sb("ot", [P, 2, 512])
        rc = sb("rc", [P, 2, 4, HG])
        mparts = sb("mparts", [P, SLOTS, HG, TB, 2])
        nmax = sb("nmax", [P, SLOTS, HG * TB])
        nrow = sb("nrow", [HG * TB, 2, P])
        nparts = sb("nparts", [HG * TB, SLOTS, 3, P], BF16)

        logit = sb("logit", [P, NT, E])
        lmax = sb("lmax", [P, NT])
        eq = sb("eq", [P, NT, E])
        onehot = sb("onehot", [P, NT, E])
        used = sb("used", [P, 2, NT])

        scr = [[nc.dram_tensor(f"scr{n}{k}", [3, B, C, T], BF16, kind="Internal").ap() for k in "qk"]
               for n in range(2)]

        done = {k: sem("done_" + k) for k in STEP_KINDS if k not in (
            "scores", "max", "store", "load", "rows", "out", "quiet", "weights", "turn", "turnmax",
            "b2_parts", "combine")}
        x_in = [sem(f"x_in{n}") for n in range(NB)]
        wqkv_in, geo_in, w_in, cs_in, moe_in, b2_in = (
            sem(n) for n in ("wqkv_in", "geo_in", "w_in", "cs_in", "moe_in", "b2_in"))
        made = sem("made")
        dchain, gchain = sem("dchain"), sem("gchain")
        wk_made, b2_split, b2_moved = sem("wk_made"), sem("b2_split"), sem("b2_moved")
        scored, exped = sem("scored"), sem("exped")
        given, taken = sem("given"), sem("taken")
        combined = sem("combined")
        ns_hi, ns_mid, np_ready = sem("ns_hi"), sem("ns_mid"), sem("np_ready")
        rc_done = sem("rc_done")
        stored = [sem(f"stored{i}") for i in range(PARTS)]
        qk_in = [sem(f"qk_in{i}") for i in range(SLOTS)]
        rows_in, out_done = sem("rows_in"), sem("out_done")

        block = ctx.enter_context(nc.Block())

        def loaded(F):
            return sum(32 * len(GROUPS[G][0].products) for G in range(F % SLOTS, F + 1, SLOTS))

        def stored_value(M):
            return 16 * (M // PARTS + 1)

        def scores_at(F, v):
            s, _, nh = UNITS[v]
            bank = ps[:, SCB + (F * NU + v) % SCN, 0:nh * STEPS[s][3]]
            return bank.rearrange("p (h n) -> p h n", h=nh)

        def turn_bank(*step):
            return ps[:, MAXB + TURN_OF[step] % MAXN, :]

        def maxes_at(F, u):
            _, _, _, nh, w = MAXES[u]
            return turn_bank("max", F, u)[:, 0:nh * w].rearrange("p (h w) -> p h w", h=nh)

        def by_group(at, b):
            return vall[:, b * T:(b + 1) * T].rearrange("p (g i w) -> p g i w", g=at.gb, i=TB)

        def side(*step):
            return ps[:, BANK_OF[step], :]

        def tiles(t, b, i):
            return t[:, TB * b + 4 * i:TB * b + 4 * i + 4, :]

        def columns(b, i):
            return slice(b * T + i * 512, b * T + i * 512 + 512)

        @block.sync
        def _(sp):
            x_view = a["x"].rearrange("b (t p) c -> p (b t) c", p=P)
            for n in range(NB):
                sp.dma_start(x0[:, 4 * n:4 * n + 4, :], x_view[:, 4 * n:4 * n + 4, :]).then_inc(x_in[n], 16)
                if n == 0:
                    sp.dma_start(w_qkv[:, :], a["w_qkv"]).then_inc(wqkv_in, 16)
                    sp.dma_start(hs[:, :], a["hs"]).then_inc(geo_in, 16)
                    sp.dma_start(sign[:, :, :], a["sign"].rearrange("p (h j) -> p h j", j=3)).then_inc(geo_in, 16)

            def weights():
                for dst, src in [(w_out[:, :], "w_out"), (wq2[:, 0, :], "WqT"), (wdkv[:, :], "WdkvT"),
                                 (wuk[:, 0, :], "WukT"), (wuv[:, :], "WuvT"), (wo[:, :], "WoT"),
                                 (norm_w[:, 0:1], "norm1"), (norm_w[:, 1:2], "norm2"),
                                 (ln_gb[:, 0:1], "ln_g"), (ln_gb[:, 1:2], "ln_b"),
                                 (gate_w[:, :], "gateT"), (gate_b[:, :], "gate_b")]:
                    sp.dma_start(dst, a[src]).then_inc(w_in, 16)
                sp.dma_start(b2, a["b2"]).then_inc(b2_in, 16)
                sp.dma_start(cos[:, :], a["cos"]).then_inc(cs_in, 16)
                sp.dma_start(sin[:, :], a["sin"]).then_inc(cs_in, 16)
                for dst, src in [(w1[:, :], "W1T"), (w2[:, :, :], "W2T"), (b1[:, :], "b1T")]:
                    sp.dma_start(dst, a[src]).then_inc(moe_in, 16)

            def move_b2():
                sp.wait_ge(b2_split, 3)
                for p in range(3):
                    sp.dma_start(b2p[p:p + 1, :], b2s[:, p, :]).then_inc(b2_moved, 16)

            def store(M):
                n, b, k, i = split_block(M)
                sp.wait_ge(done["lo"], nth("lo", M))
                dst = scr[n][k][:, b, :, i * 512:(i + 1) * 512]
                sp.dma_start(dst.rearrange("a c t -> c a t"), parts[:, M % PARTS, :, :]).then_inc(stored[M % PARTS], 16)

            def load(F):
                at, g = GROUPS[F]
                first = 8 * at.n + 4 * (g // at.gb)
                for M in range(first, first + 4):
                    sp.wait_ge(stored[M % PARTS], stored_value(M))
                if F >= SLOTS:
                    sp.wait_ge(scored, (F - SLOTS + 1) * NU)
                for k, dst in enumerate((qs, ks)):
                    for j, pair in enumerate(at.products):
                        src = scr[at.n][k][pair[k]].rearrange("b c t -> (b c) t")[g * at.gw:(g + 1) * at.gw, :]
                        sp.dma_start(dst[j * at.hd:(j + 1) * at.hd, F % SLOTS, :, :],
                                     src.rearrange("(h d) t -> d h t", d=at.hd)).then_inc(qk_in[F % SLOTS], 16)

            def rows(F):
                sp.wait_ge(np_ready, F + 1)
                for p in range(3):
                    sp.dma_start(qs[KMAX + p:KMAX + p + 1, F % SLOTS, :, :].rearrange("a h t -> a (h t)"),
                                 nparts[:, F % SLOTS, p, :]).then_inc(rows_in, 16)

            o_view = out.rearrange("b (t p) c -> p (b t) c", p=P)
            for kind, *args in SCHEDULE:
                if kind == "store":
                    store(*args)
                elif kind == "load":
                    load(*args)
                elif kind == "rows":
                    rows(*args)
                elif kind == "weights":
                    weights()
                elif kind == "b2_parts":
                    move_b2()
                elif kind == "out":
                    b, i = args
                    sp.wait_ge(done["layer_norm"], nth("layer_norm", 2, b, i))
                    sp.dma_start(tiles(o_view, b, i), tiles(xn, b, i)).then_inc(out_done, 16)
            sp.wait_ge(out_done, 16 * NB)

        @block.gpsimd
        def _(pool):
            pool.memset(ident[:, :], 0.0).then_inc(gchain, 1)
            pool.memset(identb[:, :], 0.0).then_inc(gchain, 1)
            pool.memset(cmask[:, :, :], 0.0).then_inc(gchain, 1)
            pool.wait_ge(gchain, 3)
            for t in (ident, identb):
                pool.affine_select(out=t[:, :], in_=t[:, :], compare_op=ALU.not_equal, fill=1.0,
                                   base=0, pattern=[[-1, P]], channel_multiplier=1).then_inc(made, 1)
            pool.affine_select(out=cmask[:, :, :], in_=cmask[:, :, :], compare_op=ALU.is_ge, fill=NEG,
                               base=0, pattern=[[0, HG], [-1, P]], channel_multiplier=1).then_inc(made, 1)
            pool.memset(mparts[:, :, :, 0:4, 1], -3.0e38).then_inc(made, 1)
            pool.memset(vs[:, :, :, :], 0.0).then_inc(made, 1)
            pool.wait_ge(made, 5)
            vh = vs[:, :, :, :].rearrange("p s t (h v) -> p (s t h) v", v=VW)
            pool.memset(vh[:, :, 0:1], 1.0).then_inc(made, 1)
            pool.wait_ge(made, 6)
            pool.memset(ones3[:, :], 1.0).then_inc(made, 1)
            pool.wait_ge(made, 7)

            before = [made, 7]

            def pads(slot):
                pool.wait_ge(*before)
                pool.memset(ks[KMAX:KEXP, slot, :, :], 1.0).then_inc(done["pads"], 1)
                pool.wait_ge(done["pads"], nth("pads", slot))

            def zeros(F):
                pool.wait_ge(scored, (F - SLOTS + 1) * NU)
                pool.wait_ge(*before)
                pool.memset(qs[ATT[1].kprod:KMAX, F % SLOTS, :, :], 0.0).then_inc(done["zeros"], 1)
                pool.wait_ge(done["zeros"], nth("zeros", F))

            def copy_v(F):
                at, g = GROUPS[F]
                b = g // at.gb
                pool.wait_ge(done["v_out"], nth("v_out", at.n, b, 1))
                if F >= VSLOTS:
                    pool.wait_ge(done["pv"], nth("pv", F - VSLOTS, NS - 1))
                dst = vs[:, F % VSLOTS, :, :].rearrange("p t (h v) -> p t h v", v=VW)[:, :, :, 1:1 + at.hd]
                src = by_group(at, b)[:, g % at.gb, :, :].rearrange("p i (h d) -> p i h d", h=HG)
                pool.tensor_copy(dst, src).then_inc(done["copy_v"], 1)

            def mask(F, s):
                p = pr[:, s % PSLOTS, :, 0:P]
                pool.wait_ge(exped, nth("scores", F, LAST_UNIT[s]))
                pool.affine_select(out=p, in_=p, compare_op=ALU.is_ge, fill=0.0, base=0,
                                   pattern=[[0, HG], [1, P]], channel_multiplier=-1).then_inc(done["mask"], 1)

            for step in SCHEDULE:
                kind, *args = step
                if kind == "pads":
                    pads(*args)
                elif kind == "zeros":
                    zeros(*args)
                elif kind == "copy_v":
                    copy_v(*args)
                elif kind == "mask":
                    mask(*args)
                elif kind == "rotated":
                    M, = args
                    pool.wait_ge(done["rotate"], nth("rotate", M, 1))
                    if M > 8:
                        pool.wait_ge(done["r1"], nth("r1", M - 1))
                    pool.tensor_tensor(rope[:, 2, :], rope[:, 0, :], rope[:, 1, :], ALU.add).then_inc(done["rotated"], 1)
                elif kind == "r1" and args[0] >= 8:
                    M, = args
                    pool.wait_ge(done["hi"], nth("hi", M))
                    pool.wait_ge(done["lo"], nth("lo", M - 2))
                    pool.tensor_tensor(rest[:, M % 2, :], rope[:, 2, :], parts[:, M % PARTS, 0, :],
                                       ALU.subtract).then_inc(done["r1"], 1)
                elif kind == "lo":
                    M, = args
                    pool.wait_ge(done["mid"], nth("mid", M))
                    pool.tensor_tensor(parts[:, M % PARTS, 2, :], rest[:, M % 2, :], parts[:, M % PARTS, 1, :],
                                       ALU.subtract).then_inc(done["lo"], 1)
                elif kind == "hat":
                    n, b, i = args
                    pool.wait_ge(done["rms_rec"], nth("rms_rec", n, b))
                    t0 = TB * b + 4 * i
                    pool.tensor_tensor(tiles(xn, b, i), tiles((x1, x0)[n], b, i),
                                       rstd[:, 4, t0:t0 + 4].unsqueeze(2).broadcast_to([P, 4, C]),
                                       ALU.mult).then_inc(done["hat"], 1)
                elif kind == "x12":
                    b, i = args
                    pool.wait_ge(done["hat"], nth("hat", 1, b, i))
                    pool.tensor_tensor(tiles(x0, b, i), tiles(x0, b, i), tiles(x1, b, i), ALU.add).then_inc(done["x12"], 1)
                else:
                    continue
                before[:] = [done[kind], nth(*step)]

        @block.tensor
        def _(pe):
            def wait_bank(*step):
                if step in FREED_BY:
                    reader = FREED_BY[step]
                    pe.wait_ge(done[reader[0]], nth(*reader))

            def maxima(F, u):
                i, c, h0, nh, w = MAXES[u]
                bank = maxes_at(F, u)
                if F == 0 and u == 0:
                    pe.wait_ge(done["r1"], nth("r1", 7))
                    pe.wait_ge(done["v_out"], nth("v_out", 0, 1, 1))
                    pe.wait_ge(made, 7)
                if u == 0:
                    pe.wait_ge(qk_in[F % SLOTS], loaded(F))
                    if ("zeros", F) in NTH:
                        pe.wait_ge(done["zeros"], nth("zeros", F))
                if TURN_OF["max", F, u] > MAXN:
                    pe.wait_ge(taken, TURN_OF["max", F, u] - MAXN)
                diagonal = 512 * c + w == (i + 1) * P
                if diagonal:
                    pe.matmul(bank[:, :, w - P:w], identb[:, :], cmask[:, 0:nh, :], start=True, stop=False,
                              skip_group_check=True)
                for h in range(nh):
                    last = pe.matmul(bank[:, h, :], qs[0:KMAX, F % SLOTS, h0 + h, i * P:(i + 1) * P],
                                     ks[0:KMAX, F % SLOTS, h0 + h, 512 * c:512 * c + w],
                                     start=not diagonal, stop=True, skip_group_check=True)
                last.then_inc(given, 1)

            def scores(F, v):
                st, h0, nh = UNITS[v]
                qb, j, lo, n, _ = STEPS[st]
                if v == 0:
                    pe.wait_ge(rows_in, 48 * (F + 1))
                    if ("pads", F) in NTH:
                        pe.wait_ge(done["pads"], nth("pads", F))
                if F or v >= SCN:
                    pe.wait_ge(exped, nth("scores", F, v) - SCN)
                to = scores_at(F, v)
                for h in range(nh):
                    last = pe.matmul(to[:, h, :], ks[0:KEXP, F % SLOTS, h0 + h, j * P:(j + 1) * P],
                                     qs[0:KEXP, F % SLOTS, h0 + h, qb * 512 + lo:qb * 512 + lo + n],
                                     start=True, stop=True)
                last.then_inc(scored, 1)

            def weigh(F, st):
                qb, j, lo, n, diagonal = STEPS[st]
                if st == 0:
                    pe.wait_ge(done["copy_v"], nth("copy_v", F))
                if j == 4 * qb and (F or qb):
                    pe.wait_ge(done["evac"], nth("evac", F, qb) - 1)
                pe.wait_ge(exped, nth("scores", F, LAST_UNIT[st]))
                if diagonal:
                    pe.wait_ge(done["mask"], nth("mask", F, st))
                for h in range(HG):
                    last = pe.matmul(ps[VW * h:VW * (h + 1), PVB, lo:lo + n],
                                     vs[:, F % VSLOTS, j, VW * h:VW * (h + 1)], pr[:, st % PSLOTS, h, 0:n],
                                     start=(j == 4 * qb), stop=(st == END[qb]), skip_group_check=True)
                last.then_inc(done["pv"], 1)

            def turn(F, q):
                pe.wait_ge(done["evac"], nth("evac", F, q))
                pe.wait_ge(taken, TURN_OF["turn", F, q] - MAXN)
                bank = turn_bank("turn", F, q)
                for t in range(4):
                    last = pe.transpose(bank[:, t * P:(t + 1) * P], ot[:, q, t * P:(t + 1) * P], ident[:, :])
                last.then_inc(given, 1)

            def turn_max(F):
                pe.wait_ge(combined, F + 1)
                pe.wait_ge(taken, TURN_OF["turnmax", F] - MAXN)
                pe.transpose(turn_bank("turnmax", F)[0:HG * TB, 0:P], nmax[:, F % SLOTS, :], ident[:, :]).then_inc(given, 1)

            def feed(src, b, i):
                if src == "x":
                    pe.wait_ge(x_in[2 * b + i], 16)
                    tile = [x0[:, TB * b + 4 * i + t, :] for t in range(4)]
                elif src[:3] == "att":
                    at = ATT[int(src[3])]
                    F = GROUPS.index((at, at.gb * (b + 1) - 1))
                    pe.wait_ge(taken, TURN_OF["turn", F, 1])
                    tile = [att[:, 4 * i + t, b * C:(b + 1) * C] for t in range(4)]
                else:
                    pe.wait_ge(done["hat"], nth("hat", int(src[3]), b, i))
                    tile = [xn[:, TB * b + 4 * i + t, :] for t in range(4)]
                wait_bank("feed", src, b, i)
                bank = side("feed", src, b, i)
                for t in range(4):
                    last = pe.transpose(bank[:, t * P:(t + 1) * P], tile[t], ident[:, :])
                last.then_inc(done["feed"], 1)

            def project(M, half):
                n, b, k, i = split_block(M)
                if n == 0:
                    pe.wait_ge(done["feat"], nth("feat", "x", b, i))
                    if k == 1:
                        pe.wait_ge(wk_made, 1)
                    weight, src = (wk[:, :] if k else w_qkv[:, 0:C]), feat[:, columns(b, i)]
                elif k == 0:
                    pe.wait_ge(done["feat"], nth("feat", "hat0", b, i))
                    pe.wait_ge(done["partners"], 1)
                    weight, src = wq2[:, half, :], feat[:, columns(b, i)]
                else:
                    pe.wait_ge(done["lat_feat"], nth("lat_feat", b, i))
                    weight, src = wuk[:, half, :], latT[:, i * 512:(i + 1) * 512]
                wait_bank("proj", M, half)
                pe.matmul(side("proj", M, half), weight, src, start=True, stop=True).then_inc(done["proj"], 1)

            def by_tiles(step, src, weight, width=C, tiles=4):
                wait_bank(*step)
                for t in range(tiles):
                    last = pe.matmul(side(*step)[:, t * width:(t + 1) * width], src[:, t * P:(t + 1) * P], weight,
                                     start=True, stop=True)
                last.then_inc(done[step[0]], 1)

            def expert(b, i, e):
                bank = side("expert", b, i, e)
                wait_bank("expert", b, i, e)
                pe.wait_ge(done["relu"], nth("relu", b, i, e * HC + HC - 1))
                for t in range(4):
                    pe.matmul(bank[:, t * P:(t + 1) * P], ones3[0:3, :], b2p[0:3, e * C:(e + 1) * C],
                              start=True, stop=False, skip_group_check=True)
                    for c in range(HC):
                        last = pe.matmul(bank[:, t * P:(t + 1) * P], hid[:, e % 2, c, t * P:(t + 1) * P],
                                         w2[:, e * HC + c, :], start=False, stop=(c == HC - 1), skip_group_check=True)
                last.then_inc(done["expert"], 1)

            pe.wait_ge(made, 3)
            pe.wait_ge(wqkv_in, 16)
            for step in SCHEDULE:
                kind, *args = step
                if kind == "max":
                    maxima(*args)
                elif kind == "scores":
                    scores(*args)
                elif kind == "pv":
                    weigh(*args)
                elif kind == "turn":
                    turn(*args)
                elif kind == "turnmax":
                    turn_max(*args)
                elif kind == "feed":
                    feed(*args)
                elif kind == "proj":
                    project(*args)
                elif kind == "v_proj":
                    n, b, i = args
                    if n == 0:
                        pe.wait_ge(done["feat"], nth("feat", "x", b, i))
                        by_tiles(step, feat[:, columns(b, i)], w_qkv[:, 2 * C:3 * C])
                    else:
                        pe.wait_ge(done["lat_feat"], nth("lat_feat", b, i))
                        by_tiles(step, latT[:, i * 512:(i + 1) * 512], wuv[:, :])
                elif kind == "y":
                    n, b, i = args
                    pe.wait_ge(w_in, 16 * 12)
                    pe.wait_ge(done["feat"], nth("feat", f"att{n}", b, i))
                    by_tiles(step, feat[:, columns(b, i)], (w_out, wo)[n][:, :])
                elif kind == "latent":
                    b, = args
                    pe.wait_ge(done["feat"], nth("feat", "hat0", b, 1))
                    by_tiles(step, feat[:, b * T:(b + 1) * T], wdkv[:, :], LAT, TB)
                elif kind == "lat_turn":
                    b, i = args
                    pe.wait_ge(done["lat_norm"], nth("lat_norm", b))
                    wait_bank(*step)
                    for t in range(4):
                        last = pe.transpose(side(*step)[0:LAT, t * P:(t + 1) * P], lat[:, 4 * i + t, :], ident[:, :])
                    last.then_inc(done["lat_turn"], 1)
                elif kind == "gate":
                    b, = args
                    pe.wait_ge(done["feat"], nth("feat", "hat1", b, 1))
                    by_tiles(step, feat[:, b * T:(b + 1) * T], gate_w[:, :], E, TB)
                    if b == 0:
                        pe.wait_ge(moe_in, 16 * 3)
                        pe.wait_ge(b2_moved, 16 * 3)
                elif kind == "hidden":
                    b, i, c = args
                    wait_bank(*step)
                    pe.matmul(side(*step), w1[:, c * P:(c + 1) * P], feat[:, columns(b, i)],
                              start=True, stop=True).then_inc(done["hidden"], 1)
                elif kind == "expert":
                    expert(*args)
                elif kind == "quiet":
                    pe.wait_ge(exped, NF * NU)
                    pe.wait_ge(done["evac"], NF * 2)
                    pe.wait_ge(taken, len(TURN_OF))

        @block.scalar
        def _(act):
            for step in SCHEDULE:
                kind, *args = step
                if kind == "scores":
                    F, v = args
                    st, h0, nh = UNITS[v]
                    if h0 == 0 and F * NS + st >= PSLOTS:
                        act.wait_ge(done["pv"], F * NS + st - PSLOTS + 1)
                    act.wait_ge(scored, nth("scores", F, v))
                    act.activation(pr[:, st % PSLOTS, h0:h0 + nh, 0:STEPS[st][3]], scores_at(F, v), ACT.Exp,
                                   scale=GROUPS[F][0].scale).then_inc(exped, 1)
                elif kind == "evac":
                    F, q = args
                    act.wait_ge(done["pv"], nth("pv", F, END[q]))
                    act.copy(ot[:, q, :], ps[:, PVB, :]).then_inc(done["evac"], 1)
                elif kind == "feat":
                    src, b, i = args
                    act.wait_ge(done["feed"], nth("feed", src, b, i))
                    dst, bank = feat[:, columns(b, i)], side("feed", src, b, i)
                    if src[:3] == "hat":
                        act.wait_ge(w_in, 16 * 12)
                        act.activation(dst, bank, ACT.Identity, scale=norm_w[:, int(src[3]):int(src[3]) + 1]).then_inc(done["feat"], 1)
                    else:
                        act.copy(dst, bank).then_inc(done["feat"], 1)
                elif kind == "hi":
                    M, = args
                    if M < 8:
                        act.wait_ge(done["proj"], nth("proj", M, 0))
                    else:
                        act.wait_ge(done["rotated"], nth("rotated", M))
                    if M >= PARTS:
                        act.wait_ge(stored[M % PARTS], stored_value(M - PARTS))
                    if M == 8:
                        act.wait_ge(b2_moved, 16 * 3)
                    act.copy(parts[:, M % PARTS, 0, :], side("proj", M, 0) if M < 8 else rope[:, 2, :]).then_inc(done["hi"], 1)
                elif kind == "mid":
                    M, = args
                    act.wait_ge(done["r1"], nth("r1", M))
                    act.copy(parts[:, M % PARTS, 1, :], rest[:, M % 2, :]).then_inc(done["mid"], 1)
                elif kind == "v_out":
                    n, b, i = args
                    at = ATT[n]
                    act.wait_ge(done["v_proj"], nth("v_proj", n, b, i))
                    if n == 1:
                        F = ATT[0].gb * (b + 1) - 1
                        act.wait_ge(done["copy_v"], nth("copy_v", F))
                    bank = side("v_proj", n, b, i)
                    act.copy(by_group(at, b)[:, :, 4 * i:4 * i + 4, :],
                             bank.rearrange("p (i g w) -> p g i w", i=4, g=at.gb)).then_inc(done["v_out"], 1)
                elif kind == "square":
                    n, b, i = args
                    if n == 0:
                        act.wait_ge(done["layer_norm"], nth("layer_norm", 0, b, i))
                    else:
                        act.wait_ge(done["residual"], nth("residual", 1, b, i))
                    act.activation(feat[:, columns(b, i)].rearrange("p (t c) -> p t c", c=C),
                                   tiles((x1, x0)[n], b, i), ACT.Square).then_inc(done["square"], 1)
                elif kind == "lat_copy":
                    b, = args
                    act.wait_ge(done["latent"], nth("latent", b))
                    act.copy(lat[:, :, :], side("latent", b).rearrange("p (t l) -> p t l", l=LAT)).then_inc(done["lat_copy"], 1)
                elif kind == "lat_feat":
                    b, i = args
                    act.wait_ge(done["lat_turn"], nth("lat_turn", b, i))
                    act.activation(latT[:, i * 512:(i + 1) * 512], side("lat_turn", b, i)[0:LAT, :], ACT.Identity,
                                   scale=ln_gb[:, 0:1], bias=ln_gb[:, 1:2]).then_inc(done["lat_feat"], 1)
                elif kind == "relu":
                    b, i, c = args
                    if (b, i, c) == (0, 0, 0):
                        act.wait_ge(done["lo"], nth("lo", 15))
                    if c % HC == 0 and nth("expert", b, i, c // HC) > 2:
                        act.wait_ge(done["expert"], nth("expert", b, i, c // HC) - 2)
                    act.wait_ge(done["hidden"], nth("hidden", b, i, c))
                    act.activation(hid[:, c // HC % 2, c % HC, :], side("hidden", b, i, c), ACT.Relu,
                                   bias=b1[:, c:c + 1]).then_inc(done["relu"], 1)

        @block.vector
        def _(dve):
            linked = [0]

            def link(ins):
                linked[0] += 1
                ins.then_inc(dchain, 1)
                dve.wait_ge(dchain, linked[0])

            def combine(F):
                dve.wait_ge(taken, TURN_OF["max", F, NX - 1])
                dve.tensor_reduce(nmax[:, F % SLOTS, :], mparts[:, F % SLOTS, :, :, :].rearrange("p h i c -> p (h i) c"),
                                  AX_X, ALU.max, negate=True).then_inc(combined, 1)

            def split_max(F):
                index = TURN_OF["turnmax", F]
                src, np = turn_bank("turnmax", F)[0:HG * TB, 0:P], nparts[:, F % SLOTS, :, :]
                dve.wait_ge(given, index)
                dve.tensor_copy(np[:, 0, :], src).then_inc(ns_hi, 1)
                dve.wait_ge(ns_hi, F + 1)
                dve.tensor_tensor(nrow[:, 0, :], src, np[:, 0, :], ALU.subtract).then_inc(taken, 1)
                dve.wait_ge(taken, index)
                dve.tensor_copy(np[:, 1, :], nrow[:, 0, :]).then_inc(ns_mid, 1)
                dve.wait_ge(ns_mid, F + 1)
                dve.tensor_tensor(np[:, 2, :], nrow[:, 0, :], np[:, 1, :], ALU.subtract).then_inc(np_ready, 1)

            def normalise(F, q):
                at, g = GROUPS[F]
                src = turn_bank("turn", F, q).rearrange("p (t h v) -> p t h v", t=4, h=HG)
                dve.wait_ge(given, TURN_OF["turn", F, q])
                dve.reciprocal(rc[:, q, :, :], src[:, :, :, 0]).then_inc(rc_done, 1)
                dve.wait_ge(rc_done, 2 * F + q + 1)
                dst = att[:, 4 * q:4 * q + 4, g * at.gw:(g + 1) * at.gw].rearrange("p i (h d) -> p i h d", h=HG)
                w = rc[:, q, :, :].unsqueeze(3).broadcast_to([P, 4, HG, at.hd])
                dve.tensor_tensor(dst, src[:, :, :, 1:1 + at.hd], w, ALU.mult).then_inc(taken, 1)

            def moments(src, tiles):
                for t in tiles:
                    last = dve.bn_stats(stats[:, t, :], src(t))
                link(last)
                for t in tiles:
                    last = dve.bn_aggr(mv[:, t, :], stats[:, t, :])
                return last

            def inverse_root(to, src, scale, eps, b):
                t = slice(TB * b, TB * (b + 1))
                v, y, h = rstd[:, 0, t], rstd[:, to, t], rstd[:, 2, t]
                link(dve.tensor_scalar(v, src[:, t], scale, eps, ALU.mult, ALU.add))
                link(dve.tensor_scalar(h.bitcast(I32), v.bitcast(I32), 1, None, ALU.arith_shift_right))
                link(dve.tensor_scalar(y.bitcast(I32), h.bitcast(I32), -1, 0x5F3759DF, ALU.mult, ALU.add))
                for n in range(3):
                    link(dve.scalar_tensor_tensor(out=h, in0=y, scalar=-0.5, in1=y, op0=ALU.mult, op1=ALU.mult))
                    link(dve.tensor_tensor(h, h, v, ALU.mult))
                    last = dve.scalar_tensor_tensor(out=y, in0=h, scalar=1.5, in1=y, op0=ALU.add, op1=ALU.mult)
                    if n < 2:
                        link(last)
                return last

            def b2_parts():
                dve.wait_ge(b2_in, 16)
                dve.wait_ge(stored[2], stored_value(5))
                dve.tensor_copy(b2s[:, 0, :], b2).then_inc(b2_split, 1)
                dve.wait_ge(b2_split, 1)
                link(dve.tensor_tensor(b2r, b2, b2s[:, 0, :], ALU.subtract))
                dve.tensor_copy(b2s[:, 1, :], b2r).then_inc(b2_split, 1)
                dve.wait_ge(b2_split, 2)
                dve.tensor_tensor(b2s[:, 2, :], b2r, b2s[:, 1, :], ALU.subtract).then_inc(b2_split, 1)

            def partners():
                dve.wait_ge(w_in, 16 * 12)
                half = ATT[1].hd // 2
                for w in (wq2, wuk):
                    own = w[:, 0, :].rearrange("p (h d) -> p h d", d=2 * half)
                    pair = w[:, 1, :].rearrange("p (h d) -> p h d", d=2 * half)
                    link(dve.tensor_scalar(pair[:, :, 0:half], own[:, :, half:2 * half], -1.0, None, ALU.mult))
                    link(dve.tensor_copy(pair[:, :, half:2 * half], own[:, :, 0:half]))
                dve.engine_nop().then_inc(done["partners"], 1)

            def pick(b):
                t = slice(TB * b, TB * (b + 1))
                gates = side("gate", b)[:, 0:TB * E].rearrange("p (t e) -> p t e", e=E)
                dve.wait_ge(done["gate"], nth("gate", b))
                link(dve.tensor_tensor(logit[:, t, :], gates, gate_b[:, :].unsqueeze(1).broadcast_to([P, TB, E]), ALU.add))
                link(dve.tensor_reduce(lmax[:, t], logit[:, t, :], AX_X, ALU.max))
                link(dve.tensor_tensor(eq[:, t, :], logit[:, t, :], lmax[:, t].unsqueeze(2).broadcast_to([P, TB, E]), ALU.is_equal))
                link(dve.tensor_copy(onehot[:, t, 0], eq[:, t, 0]))
                for e in range(1, E):
                    before = eq[:, t, 0] if e == 1 else used[:, e % 2, t]
                    link(dve.tensor_tensor(onehot[:, t, e], eq[:, t, e], before, ALU.is_gt))
                    if e < E - 1:
                        link(dve.tensor_tensor(used[:, (e + 1) % 2, t], before, eq[:, t, e], ALU.max))
                dve.engine_nop().then_inc(done["pick"], 1)

            dve.wait_ge(wqkv_in, 16)
            dve.wait_ge(geo_in, 32)
            first3 = w_qkv[:, C:2 * C].rearrange("p (h d) -> p h d", h=8)[:, :, 0:3]
            link(dve.tensor_copy(wk[:, :], w_qkv[:, C:2 * C]))
            link(dve.tensor_tensor(geo[:, :, :], first3, sign[:, :, :], ALU.mult))
            link(dve.tensor_reduce(geot[:, :], geo[:, :, :], AX_X, ALU.add))
            link(dve.tensor_tensor(geou[:, :], geot[:, :], hs[:, :], ALU.mult))
            link(dve.tensor_scalar(geot[:, :], geou[:, :], 1.0 / (3.0 * ATT[0].scale), None, ALU.mult))
            link(dve.tensor_tensor(geo[:, :, :], sign[:, :, :], geot[:, :].unsqueeze(2).broadcast_to([P, 8, 3]), ALU.mult))
            wk3 = wk[:, :].rearrange("p (h d) -> p h d", h=8)[:, :, 0:3]
            dve.tensor_tensor(wk3, first3, geo[:, :, :], ALU.add).then_inc(wk_made, 1)

            for step in SCHEDULE:
                kind, *args = step
                if kind == "max":
                    F, u = args
                    i, c, h0, nh, _ = MAXES[u]
                    if F == 0 and u == 0:
                        dve.wait_ge(made, 7)
                    dve.wait_ge(given, TURN_OF["max", F, u])
                    dve.tensor_reduce(mparts[:, F % SLOTS, h0:h0 + nh, i, c], maxes_at(F, u),
                                      AX_X, ALU.max).then_inc(taken, 1)
                elif kind == "combine":
                    combine(*args)
                elif kind == "turnmax":
                    split_max(*args)
                elif kind == "turn":
                    normalise(*args)
                elif kind == "b2_parts":
                    b2_parts()
                elif kind == "partners":
                    partners()
                elif kind == "r1" and args[0] < 8:
                    M, = args
                    dve.wait_ge(done["hi"], nth("hi", M))
                    if M >= 2:
                        dve.wait_ge(done["lo"], nth("lo", M - 2))
                    dve.tensor_tensor(rest[:, M % 2, :], side("proj", M, 0), parts[:, M % PARTS, 0, :],
                                      ALU.subtract).then_inc(done["r1"], 1)
                elif kind == "residual":
                    n, b, i = args
                    x, to = ((x0, xn), (x1, x0))[n]
                    dve.wait_ge(done["y"], nth("y", n, b, i))
                    dve.tensor_tensor(tiles(to, b, i), tiles(x, b, i), side("y", n, b, i).rearrange("p (t c) -> p t c", c=C),
                                      ALU.add).then_inc(done["residual"], 1)
                elif kind == "moments":
                    which, b, i = args
                    if which == 0:
                        dve.wait_ge(done["residual"], nth("residual", 0, b, i))
                    else:
                        dve.wait_ge(done["pick_up"], nth("pick_up", b, i, E - 1))
                    t0 = TB * b + 4 * i
                    moments(lambda t: xn[:, t, :], range(t0, t0 + 4)).then_inc(done["moments"], 1)
                elif kind == "layer_norm":
                    which, b, i = args
                    if i == 0:
                        dve.wait_ge(done["moments"], nth("moments", which, b, 1))
                        link(inverse_root(1, mv[:, :, 1], 1.0, 1e-5, b))
                    for t in range(TB * b + 4 * i, TB * b + 4 * i + 4):
                        last = dve.tensor_scalar((xn if which else x1)[:, t, :], xn[:, t, :], mv[:, t, 0:1],
                                                 rstd[:, 1, t:t + 1], ALU.subtract, ALU.mult)
                    last.then_inc(done["layer_norm"], 1)
                elif kind == "square_sum":
                    n, b, i = args
                    dve.wait_ge(done["square"], nth("square", n, b, i))
                    t0 = TB * b + 4 * i
                    dve.tensor_reduce(rstd[:, 3, t0:t0 + 4], feat[:, columns(b, i)].rearrange("p (t c) -> p t c", c=C),
                                      AX_X, ALU.add).then_inc(done["square_sum"], 1)
                elif kind == "rms_rec":
                    n, b = args
                    dve.wait_ge(done["square_sum"], nth("square_sum", n, b, 1))
                    inverse_root(4, rstd[:, 3, :], 1.0 / C, 1e-6, b).then_inc(done["rms_rec"], 1)
                elif kind == "lat_moments":
                    b, = args
                    dve.wait_ge(done["lat_copy"], nth("lat_copy", b))
                    moments(lambda t: lat[:, t - TB * b, :], range(TB * b, TB * (b + 1))).then_inc(done["lat_moments"], 1)
                elif kind == "lat_norm":
                    b, = args
                    dve.wait_ge(done["lat_moments"], nth("lat_moments", b))
                    link(inverse_root(1, mv[:, :, 1], 1.0, 1e-5, b))
                    for t in range(TB):
                        last = dve.tensor_scalar(lat[:, t, :], lat[:, t, :], mv[:, TB * b + t, 0:1],
                                                 rstd[:, 1, TB * b + t:TB * b + t + 1], ALU.subtract, ALU.mult)
                    last.then_inc(done["lat_norm"], 1)
                elif kind == "rotate":
                    M, half = args
                    if M == 8 and half == 0:
                        dve.wait_ge(cs_in, 32)
                        dve.wait_ge(b2_split, 3)
                    if M > 8:
                        dve.wait_ge(done["rotated"], nth("rotated", M - 1))
                    dve.wait_ge(done["proj"], nth("proj", M, half))
                    i = split_block(M)[3]
                    dve.tensor_tensor(rope[:, half, :], side("proj", M, half), (cos, sin)[half][:, i * 512:(i + 1) * 512],
                                      ALU.mult).then_inc(done["rotate"], 1)
                elif kind == "pick":
                    if args[0] == 0:
                        dve.wait_ge(w_in, 16 * 12)
                    pick(*args)
                elif kind == "pick_up":
                    b, i, e = args
                    dve.wait_ge(done["expert"], nth("expert", b, i, e))
                    if e == 0:
                        dve.wait_ge(done["x12"], nth("x12", b, i))
                    else:
                        dve.wait_ge(done["pick_up"], nth("pick_up", b, i, e - 1))
                    for t in range(TB * b + 4 * i, TB * b + 4 * i + 4):
                        last = dve.scalar_tensor_tensor(out=xn[:, t, :], in0=side("expert", b, i, e)[:, (t % 4) * C:(t % 4 + 1) * C],
                                                        scalar=onehot[:, t, e:e + 1], in1=(xn if e else x0)[:, t, :],
                                                        op0=ALU.mult, op1=ALU.add)
                    last.then_inc(done["pick_up"], 1)


OUT = ((B, T, C), "float32")


def shape_constants():
    half = ATT[1].hd // 2
    inv = (np.float32(1.0) / np.power(np.float32(10000.0), np.arange(half, dtype=np.float32) / np.float32(half))).astype(np.float32)
    angle = (np.arange(T, dtype=np.float32)[None, :] * inv[:, None]).astype(np.float32)
    angle = np.tile(angle, (C // half, 1))
    signs = np.array([[(i >> 2 & 1) * 2 - 1, (i >> 1 & 1) * 2 - 1, (i & 1) * 2 - 1] for i in range(8)], np.float32)
    return {"cos": np.cos(angle), "sin": np.sin(angle), "sign": np.tile(signs.reshape(1, 24), (P, 1))}


def kernel(L0_attn_x, L0_attn_w_qkv, L0_attn_w_out, L0_attn_head_scales, L0_ffn_norm1_w, L0_ffn_norm2_w,
           L0_ffn_Wq, L0_ffn_Wdkv, L0_ffn_Wuk, L0_ffn_Wuv, L0_ffn_Wo, L0_ffn_ln_g, L0_ffn_ln_b,
           L0_ffn_gate_w, L0_ffn_gate_b, L0_ffn_W1, L0_ffn_b1, L0_ffn_W2, L0_ffn_b2):
    import concourse.bacc as bacc
    from concourse.bass_utils import run_bass_kernel_spmd

    given = {
        "x": L0_attn_x, "w_qkv": L0_attn_w_qkv, "w_out": L0_attn_w_out,
        "hs": np.broadcast_to(np.asarray(L0_attn_head_scales)[None, :], (P, 8)),
        "norm1": np.asarray(L0_ffn_norm1_w)[:, None], "norm2": np.asarray(L0_ffn_norm2_w)[:, None],
        "WqT": np.asarray(L0_ffn_Wq).T, "WdkvT": np.asarray(L0_ffn_Wdkv).T, "WukT": np.asarray(L0_ffn_Wuk).T,
        "WuvT": np.asarray(L0_ffn_Wuv).T, "WoT": np.asarray(L0_ffn_Wo).T,
        "ln_g": np.asarray(L0_ffn_ln_g)[:, None], "ln_b": np.asarray(L0_ffn_ln_b)[:, None],
        "gateT": np.asarray(L0_ffn_gate_w).T, "gate_b": np.broadcast_to(np.asarray(L0_ffn_gate_b)[None, :], (P, E)),
        "W1T": np.asarray(L0_ffn_W1).reshape(E * HID, C).T, "b1T": np.asarray(L0_ffn_b1).reshape(E * HC, P).T,
        "W2T": np.asarray(L0_ffn_W2).transpose(0, 2, 1).reshape(E * HC, P, C).transpose(1, 0, 2),
        "b2": np.asarray(L0_ffn_b2).reshape(1, E * C),
    } | shape_constants()
    nc = bacc.Bacc("TRN2", target_bir_lowering=False, num_devices=1)
    arrays, aps = {}, {}
    for name, value in given.items():
        v = np.ascontiguousarray(value)
        arrays[f"in_{name}"] = v
        aps[name] = nc.dram_tensor(f"in_{name}", v.shape, mybir.dt.from_np(v.dtype), kind="ExternalInput").ap()
    out = nc.dram_tensor("out_0", OUT[0], F32, kind="ExternalOutput").ap()
    build(nc, aps, out)
    r = run_bass_kernel_spmd(nc, [arrays], core_ids=[0])
    return r.results[0]["out_0"]
```

```python
from contextlib import ExitStack

import numpy as np

import concourse.bass as bass
from concourse import mybir

F32 = mybir.dt.float32
BF16 = mybir.dt.bfloat16
I32 = mybir.dt.int32
ALU = mybir.AluOpType
ACT = mybir.ActivationFunctionType
AX_X = mybir.AxisListType.X

P = 128
B, T, C = 2, 1024, 128
NT = B * T // P
TB = T // P
NB = B * T // 512
HG = 4
VW = 32
E, HID = 4, 512
HC = HID // P
LAT = 64
SLOTS = 3
VSLOTS = 2
PSLOTS = 4
PARTS = 3
NEG = -1.0e30


class Attention:

    def __init__(self, n, hd, products, scale):
        self.n, self.hd, self.products, self.scale = n, hd, products, scale
        self.heads = C // hd
        self.gb = self.heads // HG
        self.groups = B * self.gb
        self.gw = HG * hd
        self.kprod = len(products) * hd


ATT = [Attention(0, 16, [(0, 0), (0, 1), (1, 0), (1, 1), (0, 2), (2, 0)], 16 ** -0.5),
       Attention(1, 8, [(0, 0), (0, 1), (1, 0), (1, 1), (0, 2), (2, 0), (1, 2), (2, 1)], 8 ** -0.5)]
KMAX = 96
KEXP = KMAX + 3
GROUPS = [(at, g) for at in ATT for g in range(at.groups)]
NF = len(GROUPS)


def exp_steps():
    out = []
    for qb in range(T // 512):
        for j in [*range(4 * qb, 4 * qb + 4), *range(4 * qb)]:
            lo = max(0, (j - 4 * qb) * P)
            out.append((qb, j, lo, 512 - lo, j >= 4 * qb))
    return out


STEPS = exp_steps()
NS = len(STEPS)
END = [max(s for s in range(NS) if STEPS[s][0] == qb) for qb in range(T // 512)]


def exp_units():
    out = []
    for s, (_, _, _, n, _) in enumerate(STEPS):
        nh = min(HG, 512 // n)
        out += [(s, h, nh) for h in range(0, HG, nh)]
    return out


UNITS = exp_units()
NU = len(UNITS)
LAST_UNIT = [max(v for v in range(NU) if UNITS[v][0] == s) for s in range(NS)]
MASKED = [s for s in range(NS) if STEPS[s][4]]
NM = len(MASKED)


def max_units():
    out = []
    for i in range(TB):
        for c in range(i // 4 + 1):
            w = min(512, (i + 1) * P - 512 * c)
            nh = min(HG, 512 // w)
            out += [(i, c, h, nh, w) for h in range(0, HG, nh)]
    return out


MAXES = max_units()
NX = len(MAXES)
assert NX % 2 == 0 and NS % PSLOTS == 0
LAG = 2

SCB, SCN = 0, 2
SIDE = [2, 3]
PVB = 4
MAXB, MAXN = 5, 3


def split_block(M):
    return M // 8, M // 4 % 2, M // 2 % 2, M % 2


def backbone():
    out = []
    for u in range(NX):
        out.append((-1 + u / (NX + 6), ("max", 0, u)))
    out += [(-0.1, ("combine", 0)), (-0.09, ("turnmax", 0)), (-0.08, ("rows", 0))]
    taken = [NX] + [0] * NF
    later = []
    total = HG * sum(st[3] for st in STEPS)

    for F in range(NF + 1):
        passed = 0

        def add(step, w=0):
            nonlocal passed
            pos = F + passed / total
            out.append((pos, step))
            passed += w
            for e in later:
                e[0] -= 1
            while later and later[0][0] <= 0:
                out.append((pos, later.pop(0)[1]))
            for G in range(F + 1, min(F + 3, NF)):
                lo, hi = MAX_LATE if G == ATT[0].groups else (max(MAX_SPREAD[0], 1 - G), MAX_SPREAD[1])
                while taken[G - 1] == NX and taken[G] < min(NX, int(NX * (F + passed / total - (G - 1) - lo) / (hi - lo))):
                    out.append((pos, ("max", G, taken[G])))
                    taken[G] += 1
                    if taken[G] == NX:
                        out.append((pos, ("combine", G)))
                        for wait, what in ((2, "turnmax"), (2, "rows")):
                            later.append([wait, (what, G)])
                        later.sort(key=lambda e: e[0])

        def product(s):
            if s >= LAG or F:
                G, r = (F, s - LAG) if s >= LAG else (F - 1, s - LAG + NS)
                add(("pv", G, r))
                if r in END:
                    q = END.index(r)
                    for wait, what in ((1, "evac"), (3, "turn")):
                        later.append([wait, (what, G, q)])
                    later.sort(key=lambda e: e[0])

        for s in range(NS if F < NF else LAG):
            units = [v for v in range(NU) if UNITS[v][0] == s] if F < NF else []
            for v in units:
                add(("scores", F, v), UNITS[v][2] * STEPS[s][3])
                if v == units[min(1, len(units) - 1)]:
                    product(s)
            if not units:
                product(s)
            elif STEPS[s][4]:
                out.append((out[-1][0], ("mask", F, s)))
    out += [(NF + 0.5, e[1]) for e in later]
    return out


MAX_SPREAD = (-0.2, 0.78)
MAX_LATE = (0.4, 0.9)


def before_first(b):
    out = [("feed", "x", b, 0), ("feat", "x", b, 0), ("feed", "x", b, 1), ("feat", "x", b, 1)]
    M0 = 4 * b
    for m in range(M0, M0 + 5):
        if m < M0 + 4:
            out.append(("proj", m, 0))
        if m > M0:
            out.append(("mid", m - 1))
        if m < M0 + 4:
            out.append(("hi", m))
        if m > M0:
            out += [("lo", m - 1), ("store", m - 1)]
            if m - 1 == 1:
                out.append(("load", 0, 0))
        if m < M0 + 4:
            out.append(("r1", m))
    for i in range(2):
        out += [("v_proj", 0, b, i), ("v_out", 0, b, i)]
    return out


def root(of, b, blocks):
    return [("root", of, b, blocks, part) for part in range(4)]


def rms(n, b, blocks):
    out = [("square", n, b, i) for i in blocks] + [("square_sum", n, b, i) for i in blocks]
    out += root(f"rms{n}", b, blocks) + [("hat", n, b, i) for i in blocks]
    for i in blocks:
        if n:
            out.append(("x12", b, i))
        out += [("feed", f"hat{n}", b, i), ("feat", f"hat{n}", b, i)]
    return out


def output(n, b, blocks):
    out = []
    for i in blocks:
        out += [("feed", f"att{n}", b, i), ("feat", f"att{n}", b, i)]
    for i in blocks:
        out += [("y", n, b, i), ("residual", n, b, i)]
    return out


def both(kind, *args):
    return [(kind, *args, i) for i in range(2)]


def between(b):
    out = output(0, b, (0, 1))
    out += both("moments", 0, b) + root("x1", b, (0, 1)) + both("layer_norm", 0, b)
    out += rms(0, b, (0, 1))
    M0 = 8 + 4 * b
    tail = {}

    def block(m):
        rest = tail.pop(m - 1, [])
        own = [("proj", m, 0), ("rotate", m, 0), ("proj", m, 1), ("rotate", m, 1), ("rotated", m)]
        tail[m] = [("hi", m), ("r1", m), ("mid", m), ("lo", m), ("store", m)]
        mixed = []
        for k in range(5):
            mixed.append(own[k])
            mixed += rest[k:k + 1]
        return mixed + ([("load", ATT[0].groups, 0)] if m == 10 else [])

    out += [("latent", b, 0), ("lat_copy", b, 0), ("latent", b, 1), ("lat_copy", b, 1)]
    q0 = block(M0)
    roots = root("latent", b, (0, 1))
    out += q0[:1] + [("lat_moments", b, 0)] + q0[1:3] + [("lat_moments", b, 1)] + q0[3:4] + roots[:2] + q0[4:] + roots[2:]
    q1 = block(M0 + 1)
    out += q1[:3] + both("lat_norm", b) + q1[3:]
    for i in range(2):
        out += [("lat_turn", b, i), ("lat_feat", b, i)]
    out += block(M0 + 2) + block(M0 + 3)
    v = []
    for i in range(2):
        v += [("v_proj", 1, b, i), ("v_out", 1, b, i)]
    last = tail.pop(M0 + 3)
    for k in range(5):
        out += [last[k]] + v[k:k + 1]
    return out


def ready(b, blocks):
    out = output(1, b, blocks) + rms(1, b, blocks)
    for i in blocks:
        out += [("gate", b, i), ("pick", b, i)]
    return out


def experts(b, i):
    out = []
    for c in range(E * HC + 2):
        if c < E * HC:
            out += [("hidden", b, i, c), ("relu", b, i, c)]
        if c % HC == 1 and c > HC:
            e = c // HC - 1
            out += [("expert", b, i, e, t) for t in range(4)] + [("pick_up", b, i, e)]
    return out + [("moments", 2, b, i)] + root("result", b, (i,)) + [("layer_norm", 2, b, i), ("out", b, i)]


READER = {"feed": "feat", "y": "residual", "latent": "lat_copy", "lat_turn": "lat_feat", "v_proj": "v_out",
          "gate": "pick", "hidden": "relu", "expert": "pick_up"}


LONG = {"layer_norm": 1.5, "hat": 2.0, "lat_norm": 2.0, "moments": 1.5, "pick": 1.5}


def spread(steps, first, last):
    total, passed, out = sum(LONG.get(s[0], 1.0) for s in steps), 0, []
    for s in steps:
        out.append((first + (last - first) * passed / total, s))
        passed += LONG.get(s[0], 1.0)
    return out


def loads(position, F):
    return [(position, ("load", F, k)) for k in range(2)]


def schedule():
    out = backbone()
    out += spread(before_first(0), -3, -2) + loads(-2, 0)[1:]
    out += spread(before_first(1), -1.5, -0.5) + [(-1.0, ("copy_v", 0)), *loads(-0.45, 1)]
    out += loads(0.02, 2) + loads(1.02, 3)
    out += [(0.05, ("weights",)), (0.7, ("partners",)), (0.6, ("b2_parts",))]
    out += [(-1.005 + 0.7 * F, ("pads", F)) for F in range(SLOTS)]
    out += spread(between(0), *BETWEEN[0]) + loads(BETWEEN[0][1], 4)[1:] + loads(BETWEEN[0][1], 5)
    out += spread(between(1), *BETWEEN[1])
    for F in range(6, NF):
        out += loads(F - 2 + 0.02, F)
    out += [(F - 1 + 0.4, ("copy_v", F)) for F in range(1, NF)]
    out += [(F - 2 + 0.1, ("zeros", F)) for F in range(ATT[0].groups, ATT[0].groups + SLOTS)]
    out += spread(ready(0, (0, 1)) + experts(0, 0) + experts(0, 1), *AFTER)
    out += spread(ready(1, (0,)), *LAST) + [(12.9, ("quiet",))]
    out += spread(experts(1, 0), 13, 14) + spread(ready(1, (1,)), 13, 13.7) + spread(experts(1, 1), 14, 15)
    return [s for _, s in sorted(out, key=lambda e: e[0])]


BETWEEN = [(2.21, 3.12), (4.21, 5.95)]
AFTER = (8.21, 11.7)
LAST = (11.71, 12.4)
SCHEDULE = schedule()


def plan():
    nth, bank_of, freed_by, turn_of = {}, {}, {}, {}
    seen, reader = {}, {}
    banks, nth_use = list(range(8)), {}
    for s in SCHEDULE:
        kind = s[0]
        seen[kind] = seen.get(kind, 0) + 1
        assert s not in nth
        nth[s] = seen[kind]
        if s == ("load", 0, 1):
            banks = [0, 1] + SIDE
        elif s == ("load", 2, 0):
            banks = SIDE
        elif kind == "quiet":
            banks = list(range(8))
        if kind == "expert" and s[4]:
            bank_of[s] = bank_of[s[:4] + (0,)]
        elif kind in READER or kind == "proj":
            bank = min((b for b in banks if b not in reader or reader[b] in nth), key=lambda b: nth_use.get(b, -1))
            nth_use[bank] = len(nth)
            bank_of[s] = bank
            if bank in reader:
                freed_by[s] = reader[bank]
            if kind == "proj":
                reader[bank] = ("r1", s[1]) if s[1] < 8 else ("rotate", s[1], s[2])
            else:
                reader[bank] = (READER[kind],) + s[1:4]
        if kind == "feed" and s[1][:3] == "att":
            assert ("turn", ATT[0].groups * int(s[1][3]) + ATT[int(s[1][3])].gb * (s[2] + 1) - 1, s[3]) in nth, s
        if kind in ("max", "turn", "turnmax"):
            turn_of[s] = len(turn_of) + 1
    return nth, bank_of, freed_by, turn_of


NTH, BANK_OF, FREED_BY, TURN_OF = plan()
STEP_KINDS = sorted({s[0] for s in SCHEDULE})


def nth(*step):
    return NTH[step]


def build(nc, a, out):
    ctx = ExitStack()
    with ctx:
        def sb(name, shape, dt=F32):
            return ctx.enter_context(nc.sbuf_tensor(name, shape, dt))

        def sem(name):
            return ctx.enter_context(nc.semaphore(name))

        ps = ctx.enter_context(nc.psum_tensor("ps", [P, 8, 512], F32))

        ident = sb("ident", [P, P])
        identb = sb("identb", [P, P], BF16)
        cmask = sb("cmask", [P, HG, P], BF16)
        w_qkv = sb("w_qkv", [P, 3 * C])
        w_out = sb("w_out", [P, C])
        hs = sb("hs", [P, 8])
        sign = sb("sign", [P, 8, 3])
        geo = sb("geo", [P, 8, 3])
        geot = sb("geot", [P, 8])
        geou = sb("geou", [P, 8])
        wk = sb("wk", [P, C])
        norm_w = sb("norm_w", [P, 2])
        wq2 = sb("wq2", [P, 2, C])
        wdkv = sb("wdkv", [P, LAT])
        wuk = sb("wuk", [LAT, 2, C])
        wuv = sb("wuv", [LAT, C])
        wo = sb("wo", [P, C])
        ln_gb = sb("ln_gb", [LAT, 2])
        gate_w = sb("gate_w", [P, E])
        gate_b = sb("gate_b", [P, E])
        cos = sb("cos", [P, T])
        sin = sb("sin", [P, T])
        w1 = sb("w1", [P, E * HID])
        b1 = sb("b1", [P, E * HC])
        w2 = sb("w2", [P, E * HC, C])
        b2p = sb("b2p", [3, E * C], BF16)
        ones3 = sb("ones3", [3, P], BF16)

        x0 = sb("x0", [P, NT, C])
        x1 = sb("x1", [P, NT, C])
        xn = sb("xn", [P, NT, C])
        feat = sb("feat", [P, B * T])
        att = sb("att", [P, TB, B * C])
        stats = sb("stats", [P, NT, 6])
        mv = sb("mv", [P, NT, 2])
        rstd = sb("rstd", [P, 5, NT])
        parts = sb("parts", [P, PARTS, 3, 512], BF16)
        vall = sb("vall", [P, B * T])

        work = sb("work", [P, 2 * HC * 512])
        hid = work[:, :].rearrange("p (s c n) -> p s c n", s=2, c=HC)
        rest = work[:, 0:1024].rearrange("p (s n) -> p s n", s=2)
        rope = work[:, 1024:2560].rearrange("p (s n) -> p s n", s=3)
        lat = work[:, 2560:3072].rearrange("p (t l) -> p t l", l=LAT)
        latT = work[0:LAT, 3072:4096]
        b2, b2r = rope[0:1, 0, :], rope[0:1, 1, :]
        b2s = parts[0:1, 2, :, :]

        qs = sb("qs", [P, SLOTS, HG, T], BF16)
        ks = sb("ks", [P, SLOTS, HG, T], BF16)
        vs = sb("vs", [P, VSLOTS, TB, HG * VW])
        pr = sb("pr", [P, PSLOTS, HG, 512])
        ot = sb("ot", [P, 2, 512])
        rc = sb("rc", [P, 2, 4, HG])
        mparts = sb("mparts", [P, SLOTS, HG, TB, 2])
        nmax = sb("nmax", [P, SLOTS, HG * TB])
        nrow = sb("nrow", [HG * TB, 2, P])
        nparts = sb("nparts", [HG * TB, SLOTS, 3, P], BF16)

        logit = sb("logit", [P, NT, E])
        lmax = sb("lmax", [P, NT])
        eq = sb("eq", [P, NT, E])
        onehot = sb("onehot", [P, NT, E])
        used = sb("used", [P, 2, NT])

        scr = [[nc.dram_tensor(f"scr{n}{k}", [3, B, C, T], BF16, kind="Internal").ap() for k in "qk"]
               for n in range(2)]

        done = {k: sem("done_" + k) for k in STEP_KINDS if k not in (
            "scores", "max", "store", "load", "rows", "out", "quiet", "weights", "turn", "turnmax",
            "b2_parts", "combine")}
        x_in = [sem(f"x_in{n}") for n in range(NB)]
        wqkv_in, geo_in, w_in, cs_in, moe_in, b2_in = (
            sem(n) for n in ("wqkv_in", "geo_in", "w_in", "cs_in", "moe_in", "b2_in"))
        made = sem("made")
        dchain, gchain = sem("dchain"), sem("gchain")
        wk_made, b2_split, b2_moved = sem("wk_made"), sem("b2_split"), sem("b2_moved")
        scored, exped = sem("scored"), sem("exped")
        given, taken = sem("given"), sem("taken")
        combined = sem("combined")
        ns_hi, ns_mid, np_ready = sem("ns_hi"), sem("ns_mid"), sem("np_ready")
        rc_done = sem("rc_done")
        stored = [sem(f"stored{i}") for i in range(PARTS)]
        qk_in = [sem(f"qk_in{i}") for i in range(SLOTS)]
        rows_in, out_done = sem("rows_in"), sem("out_done")

        block = ctx.enter_context(nc.Block())

        def loaded(F):
            return sum(32 * len(GROUPS[G][0].products) for G in range(F % SLOTS, F + 1, SLOTS))

        def stored_value(M):
            return 16 * (M // PARTS + 1)

        def scores_at(F, v):
            s, _, nh = UNITS[v]
            bank = ps[:, SCB + (F * NU + v) % SCN, 0:nh * STEPS[s][3]]
            return bank.rearrange("p (h n) -> p h n", h=nh)

        def turn_bank(*step):
            return ps[:, MAXB + TURN_OF[step] % MAXN, :]

        def maxes_at(F, u):
            _, _, _, nh, w = MAXES[u]
            return turn_bank("max", F, u)[:, 0:nh * w].rearrange("p (h w) -> p h w", h=nh)

        def by_group(at, b):
            return vall[:, b * T:(b + 1) * T].rearrange("p (g i w) -> p g i w", g=at.gb, i=TB)

        def side(*step):
            return ps[:, BANK_OF[step], :]

        def tiles(t, b, i):
            return t[:, block_tiles(b, i), :]

        def block_tiles(b, i):
            return slice(TB * b + 4 * i, TB * b + 4 * i + 4)

        def columns(b, i):
            return slice(b * T + i * 512, b * T + i * 512 + 512)

        @block.sync
        def _(sp):
            x_view = a["x"].rearrange("b (t p) c -> p (b t) c", p=P)
            for n in range(NB):
                sp.dma_start(x0[:, 4 * n:4 * n + 4, :], x_view[:, 4 * n:4 * n + 4, :]).then_inc(x_in[n], 16)
                if n == 0:
                    sp.dma_start(w_qkv[:, :], a["w_qkv"]).then_inc(wqkv_in, 16)
                    sp.dma_start(hs[:, :], a["hs"]).then_inc(geo_in, 16)
                    sp.dma_start(sign[:, :, :], a["sign"].rearrange("p (h j) -> p h j", j=3)).then_inc(geo_in, 16)

            def weights():
                for dst, src in [(w_out[:, :], "w_out"), (wq2[:, 0, :], "WqT"), (wdkv[:, :], "WdkvT"),
                                 (wuk[:, 0, :], "WukT"), (wuv[:, :], "WuvT"), (wo[:, :], "WoT"),
                                 (norm_w[:, 0:1], "norm1"), (norm_w[:, 1:2], "norm2"),
                                 (ln_gb[:, 0:1], "ln_g"), (ln_gb[:, 1:2], "ln_b"),
                                 (gate_w[:, :], "gateT"), (gate_b[:, :], "gate_b")]:
                    sp.dma_start(dst, a[src]).then_inc(w_in, 16)
                sp.dma_start(b2, a["b2"]).then_inc(b2_in, 16)
                sp.dma_start(cos[:, :], a["cos"]).then_inc(cs_in, 16)
                sp.dma_start(sin[:, :], a["sin"]).then_inc(cs_in, 16)
                for dst, src in [(w1[:, :], "W1T"), (w2[:, :, :], "W2T"), (b1[:, :], "b1T")]:
                    sp.dma_start(dst, a[src]).then_inc(moe_in, 16)

            def move_b2():
                sp.wait_ge(b2_split, 3)
                for p in range(3):
                    sp.dma_start(b2p[p:p + 1, :], b2s[:, p, :]).then_inc(b2_moved, 16)

            def store(M):
                n, b, k, i = split_block(M)
                sp.wait_ge(done["lo"], nth("lo", M))
                dst = scr[n][k][:, b, :, i * 512:(i + 1) * 512]
                sp.dma_start(dst.rearrange("a c t -> c a t"), parts[:, M % PARTS, :, :]).then_inc(stored[M % PARTS], 16)

            def load(F, k):
                at, g = GROUPS[F]
                first = 8 * at.n + 4 * (g // at.gb) + 2 * k
                for M in range(first, first + 2):
                    sp.wait_ge(stored[M % PARTS], stored_value(M))
                if F >= SLOTS:
                    sp.wait_ge(scored, (F - SLOTS + 1) * NU)
                for j, pair in enumerate(at.products):
                    src = scr[at.n][k][pair[k]].rearrange("b c t -> (b c) t")[g * at.gw:(g + 1) * at.gw, :]
                    sp.dma_start((qs, ks)[k][j * at.hd:(j + 1) * at.hd, F % SLOTS, :, :],
                                 src.rearrange("(h d) t -> d h t", d=at.hd)).then_inc(qk_in[F % SLOTS], 16)

            def rows(F):
                sp.wait_ge(np_ready, F + 1)
                for p in range(3):
                    sp.dma_start(qs[KMAX + p:KMAX + p + 1, F % SLOTS, :, :].rearrange("a h t -> a (h t)"),
                                 nparts[:, F % SLOTS, p, :]).then_inc(rows_in, 16)

            o_view = out.rearrange("b (t p) c -> p (b t) c", p=P)
            for kind, *args in SCHEDULE:
                if kind == "store":
                    store(*args)
                elif kind == "load":
                    load(*args)
                elif kind == "rows":
                    rows(*args)
                elif kind == "weights":
                    weights()
                elif kind == "b2_parts":
                    move_b2()
                elif kind == "out":
                    b, i = args
                    sp.wait_ge(done["layer_norm"], nth("layer_norm", 2, b, i))
                    sp.dma_start(tiles(o_view, b, i), tiles(xn, b, i)).then_inc(out_done, 16)
            sp.wait_ge(out_done, 16 * NB)

        @block.gpsimd
        def _(pool):
            pool.memset(ident[:, :], 0.0).then_inc(gchain, 1)
            pool.memset(identb[:, :], 0.0).then_inc(gchain, 1)
            pool.memset(cmask[:, :, :], 0.0).then_inc(gchain, 1)
            pool.wait_ge(gchain, 3)
            for t in (ident, identb):
                pool.affine_select(out=t[:, :], in_=t[:, :], compare_op=ALU.not_equal, fill=1.0,
                                   base=0, pattern=[[-1, P]], channel_multiplier=1).then_inc(made, 1)
            pool.affine_select(out=cmask[:, :, :], in_=cmask[:, :, :], compare_op=ALU.is_ge, fill=NEG,
                               base=0, pattern=[[0, HG], [-1, P]], channel_multiplier=1).then_inc(made, 1)
            pool.memset(mparts[:, :, :, 0:4, 1], -3.0e38).then_inc(made, 1)
            pool.memset(vs[:, :, :, :], 0.0).then_inc(made, 1)
            pool.wait_ge(made, 5)
            vh = vs[:, :, :, :].rearrange("p s t (h v) -> p (s t h) v", v=VW)
            pool.memset(vh[:, :, 0:1], 1.0).then_inc(made, 1)
            pool.wait_ge(made, 6)
            pool.memset(ones3[:, :], 1.0).then_inc(made, 1)
            pool.wait_ge(made, 7)

            before = [made, 7]

            def pads(slot):
                pool.wait_ge(*before)
                pool.memset(ks[KMAX:KEXP, slot, :, :], 1.0).then_inc(done["pads"], 1)
                pool.wait_ge(done["pads"], nth("pads", slot))

            def zeros(F):
                pool.wait_ge(scored, (F - SLOTS + 1) * NU)
                pool.wait_ge(*before)
                pool.memset(qs[ATT[1].kprod:KMAX, F % SLOTS, :, :], 0.0).then_inc(done["zeros"], 1)
                pool.wait_ge(done["zeros"], nth("zeros", F))

            def copy_v(F):
                at, g = GROUPS[F]
                b = g // at.gb
                pool.wait_ge(done["v_out"], nth("v_out", at.n, b, 1))
                if F >= VSLOTS:
                    pool.wait_ge(done["pv"], nth("pv", F - VSLOTS, NS - 1))
                dst = vs[:, F % VSLOTS, :, :].rearrange("p t (h v) -> p t h v", v=VW)[:, :, :, 1:1 + at.hd]
                src = by_group(at, b)[:, g % at.gb, :, :].rearrange("p i (h d) -> p i h d", h=HG)
                pool.tensor_copy(dst, src).then_inc(done["copy_v"], 1)

            def mask(F, s):
                p = pr[:, s % PSLOTS, :, 0:P]
                pool.wait_ge(exped, nth("scores", F, LAST_UNIT[s]))
                pool.affine_select(out=p, in_=p, compare_op=ALU.is_ge, fill=0.0, base=0,
                                   pattern=[[0, HG], [1, P]], channel_multiplier=-1).then_inc(done["mask"], 1)

            for step in SCHEDULE:
                kind, *args = step
                if kind == "pads":
                    pads(*args)
                elif kind == "zeros":
                    zeros(*args)
                elif kind == "copy_v":
                    copy_v(*args)
                elif kind == "mask":
                    mask(*args)
                elif kind == "rotated":
                    M, = args
                    pool.wait_ge(done["rotate"], nth("rotate", M, 1))
                    if M > 8:
                        pool.wait_ge(done["r1"], nth("r1", M - 1))
                    pool.tensor_tensor(rope[:, 2, :], rope[:, 0, :], rope[:, 1, :], ALU.add).then_inc(done["rotated"], 1)
                elif kind == "r1" and args[0] >= 8:
                    M, = args
                    pool.wait_ge(done["hi"], nth("hi", M))
                    pool.wait_ge(done["lo"], nth("lo", M - 2))
                    pool.tensor_tensor(rest[:, M % 2, :], rope[:, 2, :], parts[:, M % PARTS, 0, :],
                                       ALU.subtract).then_inc(done["r1"], 1)
                elif kind == "lo" and args[0] >= 4:
                    M, = args
                    if M == 4:
                        pool.wait_ge(done["lo"], nth("lo", 3))
                    pool.wait_ge(done["mid"], nth("mid", M))
                    pool.tensor_tensor(parts[:, M % PARTS, 2, :], rest[:, M % 2, :], parts[:, M % PARTS, 1, :],
                                       ALU.subtract).then_inc(done["lo"], 1)
                elif kind == "hat":
                    n, b, i = args
                    blocks = (0, 1) if ("root", f"rms{n}", b, (0, 1), 3) in NTH else (i,)
                    pool.wait_ge(done["root"], nth("root", f"rms{n}", b, blocks, 3))
                    t0 = TB * b + 4 * i
                    pool.tensor_tensor(tiles(xn, b, i), tiles((x1, x0)[n], b, i),
                                       rstd[:, 4, t0:t0 + 4].unsqueeze(2).broadcast_to([P, 4, C]),
                                       ALU.mult).then_inc(done["hat"], 1)
                elif kind == "x12":
                    b, i = args
                    pool.wait_ge(done["hat"], nth("hat", 1, b, i))
                    pool.tensor_tensor(tiles(x0, b, i), tiles(x0, b, i), tiles(x1, b, i), ALU.add).then_inc(done["x12"], 1)
                else:
                    continue
                before[:] = [done[kind], nth(*step)]

        @block.tensor
        def _(pe):
            def wait_bank(*step):
                if step in FREED_BY:
                    reader = FREED_BY[step]
                    pe.wait_ge(done[reader[0]], nth(*reader))

            def maxima(F, u):
                i, c, h0, nh, w = MAXES[u]
                bank = maxes_at(F, u)
                if F == 0 and u == 0:
                    pe.wait_ge(done["r1"], nth("r1", 3))
                    pe.wait_ge(done["v_out"], nth("v_out", 0, 0, 1))
                    pe.wait_ge(made, 7)
                if u == 0:
                    pe.wait_ge(qk_in[F % SLOTS], loaded(F))
                    if ("zeros", F) in NTH:
                        pe.wait_ge(done["zeros"], nth("zeros", F))
                if TURN_OF["max", F, u] > MAXN:
                    pe.wait_ge(taken, TURN_OF["max", F, u] - MAXN)
                diagonal = 512 * c + w == (i + 1) * P
                if diagonal:
                    pe.matmul(bank[:, :, w - P:w], identb[:, :], cmask[:, 0:nh, :], start=True, stop=False,
                              skip_group_check=True)
                for h in range(nh):
                    last = pe.matmul(bank[:, h, :], qs[0:KMAX, F % SLOTS, h0 + h, i * P:(i + 1) * P],
                                     ks[0:KMAX, F % SLOTS, h0 + h, 512 * c:512 * c + w],
                                     start=not diagonal, stop=True, skip_group_check=True)
                last.then_inc(given, 1)

            def scores(F, v):
                st, h0, nh = UNITS[v]
                qb, j, lo, n, _ = STEPS[st]
                if F == 0 and v == 0:
                    pe.wait_ge(done["r1"], nth("r1", 7))
                    pe.wait_ge(done["v_out"], nth("v_out", 0, 1, 1))
                if v == 0:
                    pe.wait_ge(rows_in, 48 * (F + 1))
                    if ("pads", F) in NTH:
                        pe.wait_ge(done["pads"], nth("pads", F))
                if F or v >= SCN:
                    pe.wait_ge(exped, nth("scores", F, v) - SCN)
                to = scores_at(F, v)
                for h in range(nh):
                    last = pe.matmul(to[:, h, :], ks[0:KEXP, F % SLOTS, h0 + h, j * P:(j + 1) * P],
                                     qs[0:KEXP, F % SLOTS, h0 + h, qb * 512 + lo:qb * 512 + lo + n],
                                     start=True, stop=True)
                last.then_inc(scored, 1)

            def weigh(F, st):
                qb, j, lo, n, diagonal = STEPS[st]
                if st == 0:
                    pe.wait_ge(done["copy_v"], nth("copy_v", F))
                if j == 4 * qb and (F or qb):
                    pe.wait_ge(done["evac"], nth("evac", F, qb) - 1)
                pe.wait_ge(exped, nth("scores", F, LAST_UNIT[st]))
                if diagonal:
                    pe.wait_ge(done["mask"], nth("mask", F, st))
                for h in range(HG):
                    last = pe.matmul(ps[VW * h:VW * (h + 1), PVB, lo:lo + n],
                                     vs[:, F % VSLOTS, j, VW * h:VW * (h + 1)], pr[:, st % PSLOTS, h, 0:n],
                                     start=(j == 4 * qb), stop=(st == END[qb]), skip_group_check=True)
                last.then_inc(done["pv"], 1)

            def turn(F, q):
                pe.wait_ge(done["evac"], nth("evac", F, q))
                pe.wait_ge(taken, TURN_OF["turn", F, q] - MAXN)
                bank = turn_bank("turn", F, q)
                for t in range(4):
                    last = pe.transpose(bank[:, t * P:(t + 1) * P], ot[:, q, t * P:(t + 1) * P], ident[:, :])
                last.then_inc(given, 1)

            def turn_max(F):
                pe.wait_ge(combined, F + 1)
                pe.wait_ge(taken, TURN_OF["turnmax", F] - MAXN)
                pe.transpose(turn_bank("turnmax", F)[0:HG * TB, 0:P], nmax[:, F % SLOTS, :], ident[:, :]).then_inc(given, 1)

            def feed(src, b, i):
                if src == "x":
                    pe.wait_ge(x_in[2 * b + i], 16)
                    tile = [x0[:, TB * b + 4 * i + t, :] for t in range(4)]
                elif src[:3] == "att":
                    at = ATT[int(src[3])]
                    F = GROUPS.index((at, at.gb * (b + 1) - 1))
                    pe.wait_ge(taken, TURN_OF["turn", F, i])
                    tile = [att[:, 4 * i + t, b * C:(b + 1) * C] for t in range(4)]
                else:
                    pe.wait_ge(done["hat"], nth("hat", int(src[3]), b, i))
                    tile = [xn[:, TB * b + 4 * i + t, :] for t in range(4)]
                wait_bank("feed", src, b, i)
                bank = side("feed", src, b, i)
                for t in range(4):
                    last = pe.transpose(bank[:, t * P:(t + 1) * P], tile[t], ident[:, :])
                last.then_inc(done["feed"], 1)

            def project(M, half):
                n, b, k, i = split_block(M)
                if n == 0:
                    pe.wait_ge(done["feat"], nth("feat", "x", b, i))
                    if k == 1:
                        pe.wait_ge(wk_made, 1)
                    weight, src = (wk[:, :] if k else w_qkv[:, 0:C]), feat[:, columns(b, i)]
                elif k == 0:
                    pe.wait_ge(done["feat"], nth("feat", "hat0", b, i))
                    pe.wait_ge(done["partners"], 1)
                    weight, src = wq2[:, half, :], feat[:, columns(b, i)]
                else:
                    pe.wait_ge(done["lat_feat"], nth("lat_feat", b, i))
                    weight, src = wuk[:, half, :], latT[:, i * 512:(i + 1) * 512]
                wait_bank("proj", M, half)
                pe.matmul(side("proj", M, half), weight, src, start=True, stop=True).then_inc(done["proj"], 1)

            def by_tiles(step, src, weight, width=C):
                wait_bank(*step)
                for t in range(4):
                    last = pe.matmul(side(*step)[:, t * width:(t + 1) * width], src[:, t * P:(t + 1) * P], weight,
                                     start=True, stop=True)
                last.then_inc(done[step[0]], 1)

            def expert(b, i, e, t):
                to = side("expert", b, i, e, t)[:, t * P:(t + 1) * P]
                wait_bank("expert", b, i, e, t)
                pe.wait_ge(done["relu"], nth("relu", b, i, e * HC + HC - 1))
                pe.matmul(to, ones3[0:3, :], b2p[0:3, e * C:(e + 1) * C], start=True, stop=False, skip_group_check=True)
                for c in range(HC):
                    last = pe.matmul(to, hid[:, e % 2, c, t * P:(t + 1) * P], w2[:, e * HC + c, :],
                                     start=False, stop=(c == HC - 1), skip_group_check=True)
                last.then_inc(done["expert"], 1)

            pe.wait_ge(made, 3)
            pe.wait_ge(wqkv_in, 16)
            for step in SCHEDULE:
                kind, *args = step
                if kind == "max":
                    maxima(*args)
                elif kind == "scores":
                    scores(*args)
                elif kind == "pv":
                    weigh(*args)
                elif kind == "turn":
                    turn(*args)
                elif kind == "turnmax":
                    turn_max(*args)
                elif kind == "feed":
                    feed(*args)
                elif kind == "proj":
                    project(*args)
                elif kind == "v_proj":
                    n, b, i = args
                    if n == 0:
                        pe.wait_ge(done["feat"], nth("feat", "x", b, i))
                        by_tiles(step, feat[:, columns(b, i)], w_qkv[:, 2 * C:3 * C])
                    else:
                        pe.wait_ge(done["lat_feat"], nth("lat_feat", b, i))
                        by_tiles(step, latT[:, i * 512:(i + 1) * 512], wuv[:, :])
                elif kind == "y":
                    n, b, i = args
                    pe.wait_ge(w_in, 16 * 12)
                    pe.wait_ge(done["feat"], nth("feat", f"att{n}", b, i))
                    by_tiles(step, feat[:, columns(b, i)], (w_out, wo)[n][:, :])
                elif kind == "latent":
                    b, i = args
                    pe.wait_ge(done["feat"], nth("feat", "hat0", b, i))
                    by_tiles(step, feat[:, columns(b, i)], wdkv[:, :], LAT)
                elif kind == "lat_turn":
                    b, i = args
                    pe.wait_ge(done["lat_norm"], nth("lat_norm", b, i))
                    wait_bank(*step)
                    for t in range(4):
                        last = pe.transpose(side(*step)[0:LAT, t * P:(t + 1) * P], lat[:, 4 * i + t, :], ident[:, :])
                    last.then_inc(done["lat_turn"], 1)
                elif kind == "gate":
                    b, i = args
                    pe.wait_ge(done["feat"], nth("feat", "hat1", b, i))
                    by_tiles(step, feat[:, columns(b, i)], gate_w[:, :], E)
                    if (b, i) == (0, 0):
                        pe.wait_ge(moe_in, 16 * 3)
                        pe.wait_ge(b2_moved, 16 * 3)
                elif kind == "hidden":
                    b, i, c = args
                    wait_bank(*step)
                    pe.matmul(side(*step), w1[:, c * P:(c + 1) * P], feat[:, columns(b, i)],
                              start=True, stop=True).then_inc(done["hidden"], 1)
                elif kind == "expert":
                    expert(*args)
                elif kind == "quiet":
                    pe.wait_ge(exped, NF * NU)
                    pe.wait_ge(done["evac"], NF * 2)
                    pe.wait_ge(taken, len(TURN_OF))

        @block.scalar
        def _(act):
            for step in SCHEDULE:
                kind, *args = step
                if kind == "scores":
                    F, v = args
                    st, h0, nh = UNITS[v]
                    if h0 == 0 and F * NS + st >= PSLOTS:
                        act.wait_ge(done["pv"], F * NS + st - PSLOTS + 1)
                    act.wait_ge(scored, nth("scores", F, v))
                    act.activation(pr[:, st % PSLOTS, h0:h0 + nh, 0:STEPS[st][3]], scores_at(F, v), ACT.Exp,
                                   scale=GROUPS[F][0].scale).then_inc(exped, 1)
                elif kind == "evac":
                    F, q = args
                    act.wait_ge(done["pv"], nth("pv", F, END[q]))
                    act.copy(ot[:, q, :], ps[:, PVB, :]).then_inc(done["evac"], 1)
                elif kind == "feat":
                    src, b, i = args
                    act.wait_ge(done["feed"], nth("feed", src, b, i))
                    dst, bank = feat[:, columns(b, i)], side("feed", src, b, i)
                    if src[:3] == "hat":
                        act.wait_ge(w_in, 16 * 12)
                        act.activation(dst, bank, ACT.Identity, scale=norm_w[:, int(src[3]):int(src[3]) + 1]).then_inc(done["feat"], 1)
                    else:
                        act.copy(dst, bank).then_inc(done["feat"], 1)
                elif kind == "hi":
                    M, = args
                    if M < 8:
                        act.wait_ge(done["proj"], nth("proj", M, 0))
                    else:
                        act.wait_ge(done["rotated"], nth("rotated", M))
                    if M >= PARTS:
                        act.wait_ge(stored[M % PARTS], stored_value(M - PARTS))
                    if M == 8:
                        act.wait_ge(b2_moved, 16 * 3)
                    act.copy(parts[:, M % PARTS, 0, :], side("proj", M, 0) if M < 8 else rope[:, 2, :]).then_inc(done["hi"], 1)
                elif kind == "mid":
                    M, = args
                    act.wait_ge(done["r1"], nth("r1", M))
                    act.copy(parts[:, M % PARTS, 1, :], rest[:, M % 2, :]).then_inc(done["mid"], 1)
                elif kind == "v_out":
                    n, b, i = args
                    at = ATT[n]
                    act.wait_ge(done["v_proj"], nth("v_proj", n, b, i))
                    if n == 1:
                        F = ATT[0].gb * (b + 1) - 1
                        act.wait_ge(done["copy_v"], nth("copy_v", F))
                    bank = side("v_proj", n, b, i)
                    act.copy(by_group(at, b)[:, :, 4 * i:4 * i + 4, :],
                             bank.rearrange("p (i g w) -> p g i w", i=4, g=at.gb)).then_inc(done["v_out"], 1)
                elif kind == "square":
                    n, b, i = args
                    if n == 0:
                        act.wait_ge(done["layer_norm"], nth("layer_norm", 0, b, i))
                    else:
                        act.wait_ge(done["residual"], nth("residual", 1, b, i))
                    act.activation(feat[:, columns(b, i)].rearrange("p (t c) -> p t c", c=C),
                                   tiles((x1, x0)[n], b, i), ACT.Square).then_inc(done["square"], 1)
                elif kind == "lat_copy":
                    b, i = args
                    act.wait_ge(done["latent"], nth("latent", b, i))
                    act.copy(lat[:, 4 * i:4 * i + 4, :],
                             side("latent", b, i)[:, 0:4 * LAT].rearrange("p (t l) -> p t l", l=LAT)).then_inc(done["lat_copy"], 1)
                elif kind == "lat_feat":
                    b, i = args
                    act.wait_ge(done["lat_turn"], nth("lat_turn", b, i))
                    act.activation(latT[:, i * 512:(i + 1) * 512], side("lat_turn", b, i)[0:LAT, :], ACT.Identity,
                                   scale=ln_gb[:, 0:1], bias=ln_gb[:, 1:2]).then_inc(done["lat_feat"], 1)
                elif kind == "relu":
                    b, i, c = args
                    if (b, i, c) == (0, 0, 0):
                        act.wait_ge(done["lo"], nth("lo", 15))
                    if c % HC == 0 and nth("expert", b, i, c // HC, 3) > 8:
                        act.wait_ge(done["expert"], nth("expert", b, i, c // HC, 3) - 8)
                    act.wait_ge(done["hidden"], nth("hidden", b, i, c))
                    act.activation(hid[:, c // HC % 2, c % HC, :], side("hidden", b, i, c), ACT.Relu,
                                   bias=b1[:, c:c + 1]).then_inc(done["relu"], 1)

        @block.vector
        def _(dve):
            linked = [0]

            def link(ins):
                linked[0] += 1
                ins.then_inc(dchain, 1)
                dve.wait_ge(dchain, linked[0])

            def combine(F):
                dve.wait_ge(taken, TURN_OF["max", F, NX - 1])
                dve.tensor_reduce(nmax[:, F % SLOTS, :], mparts[:, F % SLOTS, :, :, :].rearrange("p h i c -> p (h i) c"),
                                  AX_X, ALU.max, negate=True).then_inc(combined, 1)

            def split_max(F):
                index = TURN_OF["turnmax", F]
                src, np = turn_bank("turnmax", F)[0:HG * TB, 0:P], nparts[:, F % SLOTS, :, :]
                dve.wait_ge(given, index)
                dve.tensor_copy(np[:, 0, :], src).then_inc(ns_hi, 1)
                dve.wait_ge(ns_hi, F + 1)
                dve.tensor_tensor(nrow[:, 0, :], src, np[:, 0, :], ALU.subtract).then_inc(taken, 1)
                dve.wait_ge(taken, index)
                dve.tensor_copy(np[:, 1, :], nrow[:, 0, :]).then_inc(ns_mid, 1)
                dve.wait_ge(ns_mid, F + 1)
                dve.tensor_tensor(np[:, 2, :], nrow[:, 0, :], np[:, 1, :], ALU.subtract).then_inc(np_ready, 1)

            def normalise(F, q):
                at, g = GROUPS[F]
                src = turn_bank("turn", F, q).rearrange("p (t h v) -> p t h v", t=4, h=HG)
                dve.wait_ge(given, TURN_OF["turn", F, q])
                dve.reciprocal(rc[:, q, :, :], src[:, :, :, 0]).then_inc(rc_done, 1)
                dve.wait_ge(rc_done, 2 * F + q + 1)
                dst = att[:, 4 * q:4 * q + 4, g * at.gw:(g + 1) * at.gw].rearrange("p i (h d) -> p i h d", h=HG)
                w = rc[:, q, :, :].unsqueeze(3).broadcast_to([P, 4, HG, at.hd])
                dve.tensor_tensor(dst, src[:, :, :, 1:1 + at.hd], w, ALU.mult).then_inc(taken, 1)

            def moments(src, tiles):
                for t in tiles:
                    last = dve.bn_stats(stats[:, t, :], src(t))
                link(last)
                for t in tiles:
                    last = dve.bn_aggr(mv[:, t, :], stats[:, t, :])
                return last

            def inverse_root(of, b, blocks, part):
                t = slice(TB * b + 4 * blocks[0], TB * b + 4 * blocks[-1] + 4)
                src, scale, eps, to = ((rstd[:, 3, t], 1.0 / C, 1e-6, 4) if of[:3] == "rms" else
                                       (mv[:, t, 1], 1.0, 1e-5, 1))
                v, y, h = rstd[:, 0, t], rstd[:, to, t], rstd[:, 2, t]
                if part == 0:
                    if of[:3] == "rms":
                        dve.wait_ge(done["square_sum"], nth("square_sum", int(of[3]), b, blocks[-1]))
                    elif of == "latent":
                        dve.wait_ge(done["lat_moments"], nth("lat_moments", b, 1))
                    else:
                        which = 0 if of == "x1" else 2
                        dve.wait_ge(done["moments"], nth("moments", which, b, blocks[-1]))
                    link(dve.tensor_scalar(v, src, scale, eps, ALU.mult, ALU.add))
                    link(dve.tensor_scalar(h.bitcast(I32), v.bitcast(I32), 1, None, ALU.arith_shift_right))
                    dve.tensor_scalar(y.bitcast(I32), h.bitcast(I32), -1, 0x5F3759DF, ALU.mult, ALU.add).then_inc(done["root"], 1)
                    return
                dve.wait_ge(done["root"], nth("root", of, b, blocks, part - 1))
                link(dve.scalar_tensor_tensor(out=h, in0=y, scalar=-0.5, in1=y, op0=ALU.mult, op1=ALU.mult))
                link(dve.tensor_tensor(h, h, v, ALU.mult))
                dve.scalar_tensor_tensor(out=y, in0=h, scalar=1.5, in1=y, op0=ALU.add, op1=ALU.mult).then_inc(done["root"], 1)

            def b2_parts():
                dve.wait_ge(b2_in, 16)
                dve.wait_ge(stored[2], stored_value(5))
                dve.tensor_copy(b2s[:, 0, :], b2).then_inc(b2_split, 1)
                dve.wait_ge(b2_split, 1)
                link(dve.tensor_tensor(b2r, b2, b2s[:, 0, :], ALU.subtract))
                dve.tensor_copy(b2s[:, 1, :], b2r).then_inc(b2_split, 1)
                dve.wait_ge(b2_split, 2)
                dve.tensor_tensor(b2s[:, 2, :], b2r, b2s[:, 1, :], ALU.subtract).then_inc(b2_split, 1)

            def partners():
                dve.wait_ge(w_in, 16 * 12)
                half = ATT[1].hd // 2
                for w in (wq2, wuk):
                    own = w[:, 0, :].rearrange("p (h d) -> p h d", d=2 * half)
                    pair = w[:, 1, :].rearrange("p (h d) -> p h d", d=2 * half)
                    link(dve.tensor_scalar(pair[:, :, 0:half], own[:, :, half:2 * half], -1.0, None, ALU.mult))
                    link(dve.tensor_copy(pair[:, :, half:2 * half], own[:, :, 0:half]))
                dve.engine_nop().then_inc(done["partners"], 1)

            def pick(b, i):
                t = block_tiles(b, i)
                gates = side("gate", b, i)[:, 0:4 * E].rearrange("p (t e) -> p t e", e=E)
                dve.wait_ge(done["gate"], nth("gate", b, i))
                link(dve.tensor_tensor(logit[:, t, :], gates, gate_b[:, :].unsqueeze(1).broadcast_to([P, 4, E]), ALU.add))
                link(dve.tensor_reduce(lmax[:, t], logit[:, t, :], AX_X, ALU.max))
                link(dve.tensor_tensor(eq[:, t, :], logit[:, t, :], lmax[:, t].unsqueeze(2).broadcast_to([P, 4, E]), ALU.is_equal))
                link(dve.tensor_copy(onehot[:, t, 0], eq[:, t, 0]))
                for e in range(1, E):
                    before = eq[:, t, 0] if e == 1 else used[:, e % 2, t]
                    link(dve.tensor_tensor(onehot[:, t, e], eq[:, t, e], before, ALU.is_gt))
                    if e < E - 1:
                        link(dve.tensor_tensor(used[:, (e + 1) % 2, t], before, eq[:, t, e], ALU.max))
                dve.engine_nop().then_inc(done["pick"], 1)

            dve.wait_ge(wqkv_in, 16)
            dve.wait_ge(geo_in, 32)
            first3 = w_qkv[:, C:2 * C].rearrange("p (h d) -> p h d", h=8)[:, :, 0:3]
            link(dve.tensor_copy(wk[:, :], w_qkv[:, C:2 * C]))
            link(dve.tensor_tensor(geo[:, :, :], first3, sign[:, :, :], ALU.mult))
            link(dve.tensor_reduce(geot[:, :], geo[:, :, :], AX_X, ALU.add))
            link(dve.tensor_tensor(geou[:, :], geot[:, :], hs[:, :], ALU.mult))
            link(dve.tensor_scalar(geot[:, :], geou[:, :], 1.0 / (3.0 * ATT[0].scale), None, ALU.mult))
            link(dve.tensor_tensor(geo[:, :, :], sign[:, :, :], geot[:, :].unsqueeze(2).broadcast_to([P, 8, 3]), ALU.mult))
            wk3 = wk[:, :].rearrange("p (h d) -> p h d", h=8)[:, :, 0:3]
            dve.tensor_tensor(wk3, first3, geo[:, :, :], ALU.add).then_inc(wk_made, 1)

            for step in SCHEDULE:
                kind, *args = step
                if kind == "max":
                    F, u = args
                    i, c, h0, nh, _ = MAXES[u]
                    if F == 0 and u == 0:
                        dve.wait_ge(made, 7)
                    dve.wait_ge(given, TURN_OF["max", F, u])
                    dve.tensor_reduce(mparts[:, F % SLOTS, h0:h0 + nh, i, c], maxes_at(F, u),
                                      AX_X, ALU.max).then_inc(taken, 1)
                elif kind == "combine":
                    combine(*args)
                elif kind == "turnmax":
                    split_max(*args)
                elif kind == "turn":
                    normalise(*args)
                elif kind == "b2_parts":
                    b2_parts()
                elif kind == "partners":
                    partners()
                elif kind == "r1" and args[0] < 8:
                    M, = args
                    dve.wait_ge(done["hi"], nth("hi", M))
                    if M >= 2:
                        dve.wait_ge(done["lo"], nth("lo", M - 2))
                    dve.tensor_tensor(rest[:, M % 2, :], side("proj", M, 0), parts[:, M % PARTS, 0, :],
                                      ALU.subtract).then_inc(done["r1"], 1)
                elif kind == "lo" and args[0] < 4:
                    M, = args
                    dve.wait_ge(done["mid"], nth("mid", M))
                    dve.tensor_tensor(parts[:, M % PARTS, 2, :], rest[:, M % 2, :], parts[:, M % PARTS, 1, :],
                                      ALU.subtract).then_inc(done["lo"], 1)
                elif kind == "residual":
                    n, b, i = args
                    x, to = ((x0, xn), (x1, x0))[n]
                    dve.wait_ge(done["y"], nth("y", n, b, i))
                    dve.tensor_tensor(tiles(to, b, i), tiles(x, b, i), side("y", n, b, i).rearrange("p (t c) -> p t c", c=C),
                                      ALU.add).then_inc(done["residual"], 1)
                elif kind == "moments":
                    which, b, i = args
                    if which == 0:
                        dve.wait_ge(done["residual"], nth("residual", 0, b, i))
                    else:
                        dve.wait_ge(done["pick_up"], nth("pick_up", b, i, E - 1))
                    t0 = TB * b + 4 * i
                    moments(lambda t: xn[:, t, :], range(t0, t0 + 4)).then_inc(done["moments"], 1)
                elif kind == "layer_norm":
                    which, b, i = args
                    of, blocks = ("result", (i,)) if which else ("x1", (0, 1))
                    dve.wait_ge(done["root"], nth("root", of, b, blocks, 3))
                    for t in range(TB * b + 4 * i, TB * b + 4 * i + 4):
                        last = dve.tensor_scalar((xn if which else x1)[:, t, :], xn[:, t, :], mv[:, t, 0:1],
                                                 rstd[:, 1, t:t + 1], ALU.subtract, ALU.mult)
                    last.then_inc(done["layer_norm"], 1)
                elif kind == "square_sum":
                    n, b, i = args
                    dve.wait_ge(done["square"], nth("square", n, b, i))
                    t0 = TB * b + 4 * i
                    dve.tensor_reduce(rstd[:, 3, t0:t0 + 4], feat[:, columns(b, i)].rearrange("p (t c) -> p t c", c=C),
                                      AX_X, ALU.add).then_inc(done["square_sum"], 1)
                elif kind == "root":
                    inverse_root(*args)
                elif kind == "lat_moments":
                    b, i = args
                    dve.wait_ge(done["lat_copy"], nth("lat_copy", b, i))
                    t0 = TB * b + 4 * i
                    moments(lambda t: lat[:, t - TB * b, :], range(t0, t0 + 4)).then_inc(done["lat_moments"], 1)
                elif kind == "lat_norm":
                    b, i = args
                    dve.wait_ge(done["root"], nth("root", "latent", b, (0, 1), 3))
                    for t in range(4 * i, 4 * i + 4):
                        last = dve.tensor_scalar(lat[:, t, :], lat[:, t, :], mv[:, TB * b + t, 0:1],
                                                 rstd[:, 1, TB * b + t:TB * b + t + 1], ALU.subtract, ALU.mult)
                    last.then_inc(done["lat_norm"], 1)
                elif kind == "rotate":
                    M, half = args
                    if M == 8 and half == 0:
                        dve.wait_ge(cs_in, 32)
                        dve.wait_ge(b2_split, 3)
                    if M > 8:
                        dve.wait_ge(done["rotated"], nth("rotated", M - 1))
                    dve.wait_ge(done["proj"], nth("proj", M, half))
                    i = split_block(M)[3]
                    dve.tensor_tensor(rope[:, half, :], side("proj", M, half), (cos, sin)[half][:, i * 512:(i + 1) * 512],
                                      ALU.mult).then_inc(done["rotate"], 1)
                elif kind == "pick":
                    if args == [0, 0]:
                        dve.wait_ge(w_in, 16 * 12)
                    pick(*args)
                elif kind == "pick_up":
                    b, i, e = args
                    dve.wait_ge(done["expert"], nth("expert", b, i, e, 3))
                    if e == 0:
                        dve.wait_ge(done["x12"], nth("x12", b, i))
                    else:
                        dve.wait_ge(done["pick_up"], nth("pick_up", b, i, e - 1))
                    for t in range(TB * b + 4 * i, TB * b + 4 * i + 4):
                        last = dve.scalar_tensor_tensor(out=xn[:, t, :], in0=side("expert", b, i, e, 0)[:, (t % 4) * C:(t % 4 + 1) * C],
                                                        scalar=onehot[:, t, e:e + 1], in1=(xn if e else x0)[:, t, :],
                                                        op0=ALU.mult, op1=ALU.add)
                    last.then_inc(done["pick_up"], 1)


OUT = ((B, T, C), "float32")


def shape_constants():
    half = ATT[1].hd // 2
    inv = (np.float32(1.0) / np.power(np.float32(10000.0), np.arange(half, dtype=np.float32) / np.float32(half))).astype(np.float32)
    angle = (np.arange(T, dtype=np.float32)[None, :] * inv[:, None]).astype(np.float32)
    angle = np.tile(angle, (C // half, 1))
    signs = np.array([[(i >> 2 & 1) * 2 - 1, (i >> 1 & 1) * 2 - 1, (i & 1) * 2 - 1] for i in range(8)], np.float32)
    return {"cos": np.cos(angle), "sin": np.sin(angle), "sign": np.tile(signs.reshape(1, 24), (P, 1))}


def kernel(L0_attn_x, L0_attn_w_qkv, L0_attn_w_out, L0_attn_head_scales, L0_ffn_norm1_w, L0_ffn_norm2_w,
           L0_ffn_Wq, L0_ffn_Wdkv, L0_ffn_Wuk, L0_ffn_Wuv, L0_ffn_Wo, L0_ffn_ln_g, L0_ffn_ln_b,
           L0_ffn_gate_w, L0_ffn_gate_b, L0_ffn_W1, L0_ffn_b1, L0_ffn_W2, L0_ffn_b2):
    import concourse.bacc as bacc
    from concourse.bass_utils import run_bass_kernel_spmd

    given = {
        "x": L0_attn_x, "w_qkv": L0_attn_w_qkv, "w_out": L0_attn_w_out,
        "hs": np.broadcast_to(np.asarray(L0_attn_head_scales)[None, :], (P, 8)),
        "norm1": np.asarray(L0_ffn_norm1_w)[:, None], "norm2": np.asarray(L0_ffn_norm2_w)[:, None],
        "WqT": np.asarray(L0_ffn_Wq).T, "WdkvT": np.asarray(L0_ffn_Wdkv).T, "WukT": np.asarray(L0_ffn_Wuk).T,
        "WuvT": np.asarray(L0_ffn_Wuv).T, "WoT": np.asarray(L0_ffn_Wo).T,
        "ln_g": np.asarray(L0_ffn_ln_g)[:, None], "ln_b": np.asarray(L0_ffn_ln_b)[:, None],
        "gateT": np.asarray(L0_ffn_gate_w).T, "gate_b": np.broadcast_to(np.asarray(L0_ffn_gate_b)[None, :], (P, E)),
        "W1T": np.asarray(L0_ffn_W1).reshape(E * HID, C).T, "b1T": np.asarray(L0_ffn_b1).reshape(E * HC, P).T,
        "W2T": np.asarray(L0_ffn_W2).transpose(0, 2, 1).reshape(E * HC, P, C).transpose(1, 0, 2),
        "b2": np.asarray(L0_ffn_b2).reshape(1, E * C),
    } | shape_constants()
    nc = bacc.Bacc("TRN2", target_bir_lowering=False, num_devices=1)
    arrays, aps = {}, {}
    for name, value in given.items():
        v = np.ascontiguousarray(value)
        arrays[f"in_{name}"] = v
        aps[name] = nc.dram_tensor(f"in_{name}", v.shape, mybir.dt.from_np(v.dtype), kind="ExternalInput").ap()
    out = nc.dram_tensor("out_0", OUT[0], F32, kind="ExternalOutput").ap()
    build(nc, aps, out)
    r = run_bass_kernel_spmd(nc, [arrays], core_ids=[0])
    return r.results[0]["out_0"]
```
